# Optimizing a Trainium2 kernel written in Bass

```python
import numpy as np
import jax
import jax.numpy as jnp

def _softmax(x, axis=-1):
    return jax.nn.softmax(x, axis=axis)

def _gelu(x):
    return jax.nn.gelu(x, approximate=True)

def _silu(x):
    return jax.nn.silu(x)

def _sigmoid(x):
    return jax.nn.sigmoid(x)

def _layernorm(x, axis=-1, eps=1e-05):
    m = jnp.mean(x, axis=axis, keepdims=True)
    v = jnp.var(x, axis=axis, keepdims=True)
    return (x - m) / jnp.sqrt(v + eps)

def _scatter_add(tgt, idx, src, axis=0):
    return tgt.at[idx].add(src)

def _segment_sum(src, seg, n):
    return jax.ops.segment_sum(src, seg, n)
kernel_name = 'mk_xattn_ffn_d1_seqx_r4_3f4de5'

def setup_inputs(seed: int=0):
    np.random.seed(seed)
    _w = jnp.asarray

    def _rec_inputs():
        import jax
        import jax.numpy as jnp
        _rk = jax.random.key(seed)
        x = -1.394e-06 + 0.9999 * jax.random.normal(jax.random.fold_in(_rk, 1), (4, 512, 256), jnp.float32)
        _lenS = 512 - jax.random.randint(jax.random.fold_in(_rk, 7), (4,), 0, max(1, 512 // 4) + 1, jnp.int32)
        _lenS2 = 512 - jax.random.randint(jax.random.fold_in(_rk, 8), (4,), 0, max(1, 512 // 4) + 1, jnp.int32)
        _ctx_1024P = jax.random.normal(jax.random.fold_in(_rk, 11), (4, 16, 256), jnp.float32)
        _ctx_1024c = jax.random.dirichlet(jax.random.fold_in(_rk, 511), 0.3 * jnp.ones((16,), jnp.float32), (4, 512))
        _ctx_1024t = jnp.einsum('bsk,bkd->bsd', _ctx_1024c, _ctx_1024P)
        _ctx_1024t = _ctx_1024t * jax.lax.rsqrt(jnp.mean(jnp.square(_ctx_1024t)) + 1e-12) * 0.953939
        ctx_1024 = -0.000292821 + 1.00034 * (_ctx_1024t + 0.3 * jax.random.normal(jax.random.fold_in(_rk, 611), (4, 512, 256), jnp.float32))
        return (x, ctx_1024)
    x, ctx_1024 = _rec_inputs()

    def _L0_xattn_setup():
        import jax, jax.numpy as jnp
        import numpy as np
        D_MODEL = 256
        N_HEAD = 16
        HEAD_DIM = D_MODEL // N_HEAD
        key = jax.random.key(seed)
        ks = jax.random.split(key, 9)
        B, T = (2, 512)
        s = 0.02
        return {'k': jax.random.normal(ks[0], (B, T, D_MODEL), jnp.float32), 'q': jax.random.normal(ks[1], (B, T, D_MODEL), jnp.float32), 'v': jax.random.normal(ks[2], (B, T, D_MODEL), jnp.float32), 'Wk': jax.random.normal(ks[3], (D_MODEL, D_MODEL), jnp.float32) * s, 'bk': jnp.zeros((D_MODEL,), jnp.float32), 'Wq': jax.random.normal(ks[4], (D_MODEL, D_MODEL), jnp.float32) * s, 'bq': jnp.zeros((D_MODEL,), jnp.float32), 'Wc': jax.random.normal(ks[5], (D_MODEL, D_MODEL), jnp.float32) * s, 'bc': jnp.zeros((D_MODEL,), jnp.float32)}
    _L0_xattn_all = _L0_xattn_setup()
    _L0_xattn_in = {k: v for k, v in _L0_xattn_all.items() if k in ('Wk', 'bk', 'Wq', 'bq', 'Wc', 'bc')}
    del _L0_xattn_all

    def _L0_ffn_setup():
        import jax, jax.numpy as jnp
        import numpy as np
        TOPK = 4
        key = jax.random.key(seed)
        ks = jax.random.split(key, 9)
        B, T, D = (4, 512, 256)
        E, H = (32, 128)
        HS = H * TOPK
        s = lambda k, shape, fan: jax.random.normal(k, shape, dtype=jnp.float32) / np.sqrt(fan)
        return {'x': jax.random.normal(ks[0], (B, T, D), dtype=jnp.float32), 'router_w': s(ks[1], (E, D), D), 'router_bias': jnp.zeros((E,), dtype=jnp.float32), 'gate_w': s(ks[2], (E, H, D), D), 'up_w': s(ks[3], (E, H, D), D), 'down_w': s(ks[4], (E, D, H), H), 'sgate_w': s(ks[5], (HS, D), D), 'sup_w': s(ks[6], (HS, D), D), 'sdown_w': s(ks[7], (D, HS), HS)}
    _L0_ffn_all = _L0_ffn_setup()
    _L0_ffn_in = {k: v for k, v in _L0_ffn_all.items() if k in ('router_w', 'router_bias', 'gate_w', 'up_w', 'down_w', 'sgate_w', 'sup_w', 'sdown_w')}
    del _L0_ffn_all
    return {'x': x, 'ctx_1024': ctx_1024, 'L0_xattn_Wk': _L0_xattn_in['Wk'], 'L0_xattn_bk': _L0_xattn_in['bk'], 'L0_xattn_Wq': _L0_xattn_in['Wq'], 'L0_xattn_bq': _L0_xattn_in['bq'], 'L0_xattn_Wc': _L0_xattn_in['Wc'], 'L0_xattn_bc': _L0_xattn_in['bc'], 'L0_ffn_router_w': _L0_ffn_in['router_w'], 'L0_ffn_router_bias': _L0_ffn_in['router_bias'], 'L0_ffn_gate_w': _L0_ffn_in['gate_w'], 'L0_ffn_up_w': _L0_ffn_in['up_w'], 'L0_ffn_down_w': _L0_ffn_in['down_w'], 'L0_ffn_sgate_w': _L0_ffn_in['sgate_w'], 'L0_ffn_sup_w': _L0_ffn_in['sup_w'], 'L0_ffn_sdown_w': _L0_ffn_in['sdown_w']}

def reference(x, ctx_1024, L0_xattn_Wk, L0_xattn_bk, L0_xattn_Wq, L0_xattn_bq, L0_xattn_Wc, L0_xattn_bc, L0_ffn_router_w, L0_ffn_router_bias, L0_ffn_gate_w, L0_ffn_up_w, L0_ffn_down_w, L0_ffn_sgate_w, L0_ffn_sup_w, L0_ffn_sdown_w):
    import jax
    import jax.numpy as jnp

    def _L0_xattn_ref(k, q, v, Wk, bk, Wq, bq, Wc, bc):
        import jax, jax.numpy as jnp
        import numpy as np
        D_MODEL = 256
        N_HEAD = 16
        HEAD_DIM = D_MODEL // N_HEAD
        B, T_v, C = v.shape
        T_q = q.shape[1]
        H, hd = (N_HEAD, C // N_HEAD)
        kp = k @ Wk.T + bk
        qp = q @ Wq.T + bq
        kh = kp.reshape(B, T_v, H, hd).transpose(0, 2, 1, 3)
        qh = qp.reshape(B, T_q, H, hd).transpose(0, 2, 1, 3)
        vh = v.reshape(B, T_v, H, hd).transpose(0, 2, 1, 3)
        scale = 1.0 / jnp.sqrt(jnp.asarray(hd, kh.dtype))
        att = jnp.einsum('bhqd,bhkd->bhqk', qh, kh) * scale
        att = jax.nn.softmax(att, axis=-1)
        y = jnp.einsum('bhqk,bhkd->bhqd', att, vh)
        y = y.transpose(0, 2, 1, 3).reshape(B, T_q, C)
        return y @ Wc.T + bc

    def _L0_ffn_ref(x, router_w, router_bias, gate_w, up_w, down_w, sgate_w, sup_w, sdown_w):
        import jax, jax.numpy as jnp
        import numpy as np
        TOPK = 4
        B, T, D = x.shape
        flat = x.reshape(B * T, D)
        logits = flat.astype(jnp.float32) @ router_w.T + router_bias
        scores = jax.nn.softmax(logits, axis=-1)
        topk_scores, topk_idx = jax.lax.top_k(scores, TOPK)
        topk_scores = topk_scores / jnp.clip(topk_scores.sum(axis=-1, keepdims=True), 1e-12, None)
        h = jax.nn.silu(jnp.einsum('nd,ehd->neh', flat, gate_w)) * jnp.einsum('nd,ehd->neh', flat, up_w)
        expert_out = jnp.einsum('neh,edh->ned', h, down_w)
        sel = jnp.take_along_axis(expert_out, topk_idx[:, :, None], axis=1)
        out = (sel * topk_scores.astype(flat.dtype)[:, :, None]).sum(axis=1)
        out = out + jax.nn.silu(flat @ sgate_w.T) * (flat @ sup_w.T) @ sdown_w.T
        return out.reshape(B, T, D)
    x = x + _L0_xattn_ref(ctx_1024, _layernorm(x, axis=-1), ctx_1024, L0_xattn_Wk, L0_xattn_bk, L0_xattn_Wq, L0_xattn_bq, L0_xattn_Wc, L0_xattn_bc)
    x = x + _L0_ffn_ref(_layernorm(x, axis=-1), L0_ffn_router_w, L0_ffn_router_bias, L0_ffn_gate_w, L0_ffn_up_w, L0_ffn_down_w, L0_ffn_sgate_w, L0_ffn_sup_w, L0_ffn_sdown_w)
    return x

_drawn_inputs = setup_inputs


def setup_inputs(seed=0):
    import zlib

    import numpy as np

    out = dict(_drawn_inputs(seed))
    spreads = {'L0_xattn_bk': (0.0, 0.8),
     'L0_xattn_bq': (0.0, 0.795),
     'L0_xattn_bc': (0.0, 0.1),
     'L0_ffn_router_bias': (0.0, 0.1)}
    factors = {'L0_xattn_Wk': 3.637, 'L0_xattn_Wq': 3.538}
    for name, (base, spread) in spreads.items():
        noise = np.random.default_rng([zlib.crc32(name.encode()), seed]).standard_normal(out[name].shape)
        drawn = base * np.exp(spread * noise) if base else spread * noise
        out[name] = jnp.asarray(drawn.astype(out[name].dtype))
    for name, factor in factors.items():
        out[name] = (out[name] * factor).astype(out[name].dtype)
    return out
```

```python
from contextlib import ExitStack

import concourse.bass as bass
from concourse import mybir

ALU = mybir.AluOpType
ACT = mybir.ActivationFunctionType
AX = mybir.AxisListType
F32 = mybir.dt.float32
BF16 = mybir.dt.bfloat16
I32 = mybir.dt.int32
U32 = mybir.dt.uint32

P = 128
B, T, D = 4, 512, 256
N = B * T
H, HD = 16, 16
C = D // P
QT = T // P
NT = N // P
E, EH, TOPK = 32, 128, 4
SH = 512
SC = SH // P
SCALE = HD ** -0.5
LN_EPS = 1e-5

Q_PART = (0, 0, 1, 0, 2, 1)
K_PART = (0, 1, 0, 2, 0, 1)
BLOCKS = len(Q_PART)
SHIFT_ROW = BLOCKS * HD
ROWS = SHIFT_ROW + 3

GH = 4
GROUPS = B * H // GH
BG = H // GH
UNITS = QT * GH
ALL = GROUPS * UNITS
AHEAD = 2 * UNITS
LAG = 4
S_BANKS, M_BANKS = 3, 2
P_RING = 8

UNROLL = 4
SLOT_TILES = -(-((N * TOPK + E * (P - 1)) // P) // UNROLL) * UNROLL
SLOTS = SLOT_TILES * P
WORDS = 3 * D
M_SLOT, M_WEIGHT, M_TOKEN, ROW = D, D + TOPK, D + 2 * TOPK, D + 2 * TOPK + 1
META = ROW - D
FILLS = 8
FILL_TILES = SLOT_TILES // FILLS
DEPTH = 3


def stage_plan():
    at = {}

    def put(slot, name, *arg):
        at.setdefault(slot, []).append((name, *arg))

    for b in range(2):
        first = -AHEAD - 8 if b == 0 else -AHEAD + 1
        for n, (name, c) in enumerate((("K", 0), ("K", 1), ("NT", 0), ("NT", 1), ("Q", 0), ("Q", 1))):
            put(first + (n if b == 0 else 3 * n), name, b, c)
    for b in range(2, B):
        s = UNITS * (BG * (b - 1) - 1)
        for u, name, c in ((2, "NT", 0), (5, "NT", 1), (9, "K", 0), (11, "K", 1), (13, "Q", 0), (15, "Q", 1)):
            put(s + u, name, b, c)
    for g in range(GROUPS):
        put(UNITS * (g - 1) + 4, "MR", g)
        put(UNITS * (g + 1) + LAG + 3, "YT", g)
    for b in range(B):
        s = UNITS * BG * (b + 1)
        for u, name, c in ((9, "AT", 0), (11, "AT", 1), (13, "WC", 0), (15, "WC", 1),
                           (25, "XT", 0), (27, "XT", 1), (29, "LG", 0)):
            put(s + u, name, b, c)
    return at


STAGES_AT = stage_plan()
FIRST_SLOT = min(STAGES_AT)
LAST_SLOT = max(STAGES_AT) + 4
ROUTE_SLOT = {b: STAGE_SLOT for b, STAGE_SLOT in ((b, UNITS * BG * (b + 1) + 29) for b in range(B))}
STAGE_NO = {}
for _s in range(FIRST_SLOT, LAST_SLOT + 1):
    for _st in STAGES_AT.get(_s, ()):
        STAGE_NO[_st] = len(STAGE_NO)


def through(*stage):
    return STAGE_NO[stage] + 1


NORM_SLOTS = {(1, 0): FIRST_SLOT, (1, 1): FIRST_SLOT + 3}
for _b in range(2, B):
    NORM_SLOTS[(1, _b)] = UNITS * (BG * (_b - 1) - 1) - 6
for _b in range(B):
    NORM_SLOTS[(2, _b)] = UNITS * BG * (_b + 1) + 17
NORM_NO = {k: n for n, k in enumerate(sorted(NORM_SLOTS, key=NORM_SLOTS.get))}
NORM_GAP = 3


def unit(n):
    g, u = divmod(n, UNITS)
    t, j = divmod(u, GH)
    return g, g // BG, g % BG * GH + j, t, j


def build(nc, x, ctxn, ctxT, wkT, wqT, wcT, bk, bq, bc, rwT, rb, sgT, suT, sdT, wall, out):
    slot_rows = nc.dram_tensor("slot_rows", (SLOTS, ROW), F32, kind="Internal").ap()
    choice_rows = nc.dram_tensor("choice_rows", (N * TOPK + SLOTS, D), F32, kind="Internal").ap()
    parts_d = nc.dram_tensor("parts", (B, 2, 3, D, T), BF16, kind="Internal").ap()
    with ExitStack() as ctx:
        def sb(name, shape, dt=F32):
            return ctx.enter_context(nc.sbuf_tensor(name, shape, dt))

        def ps(name, shape, dt=F32):
            return ctx.enter_context(nc.psum_tensor(name, shape, dt))

        def sem(name):
            return ctx.enter_context(nc.semaphore(name))

        weights = sb("weights", [P, E * WORDS])
        words = H * T // 2
        qs = [weights[:, i * words:(i + 1) * words].bitcast(BF16).rearrange("p (h t) -> p h t", h=H) for i in (0, 1)]
        ks = [weights[:, i * words:(i + 1) * words].bitcast(BF16).rearrange("p (h t) -> p h t", h=H) for i in (2, 3)]
        at = 4 * words
        vwords = QT * H * 32
        vaug = [weights[:, at + i * vwords:at + (i + 1) * vwords].rearrange("p (k h m) -> p k h m", k=QT, h=H)
                for i in (0, 1)]
        at += 2 * vwords
        expo = [weights[:, at + i * T:at + (i + 1) * T] for i in range(P_RING)]
        assert at + P_RING * T <= E * WORDS

        xres = sb("xres", [P, NT, D])
        xrow = sb("xrow", [P, NT, ROW])
        xn2T = sb("xn2T", [P, C, N])
        early = sb("early", [P, 6 * C * T])
        late = sb("late", [P, 4 * C * T])

        def cut(arena, sizes):
            at, got = 0, []
            for n in sizes:
                got.append(arena[:, at:at + n])
                at += n
            assert at <= arena.shape[1]
            return got

        def chunks(ap, n):
            return ap.rearrange("p (c n) -> p c n", c=n)

        cT, cn, xnT, full0, full1, rest, part0, part1 = cut(early, [C * T] * 3 + [T] * 3 + [3 * T // 2] * 2)
        cT, cn, xnT = chunks(cT, C), chunks(cn, QT), chunks(xnT, C)
        full = [full0, full1]
        part = [chunks(p.bitcast(BF16), 3) for p in (part0, part1)]
        o_sb, y, yT, wk, wq, wc = cut(late, [T, C * T, C * T, C * D, C * D, C * D])
        y, yT, wk, wq, wc = chunks(y, QT), chunks(yT, C), chunks(wk, C), chunks(wq, C), chunks(wc, C)

        sg, su, sd, gated0, gated1, hid = cut(early, [C * SH] * 2 + [SC * D] + [T] * 2 + [SC * T])
        sg, su, sd, hid = chunks(sg, C), chunks(su, C), chunks(sd, SC), chunks(hid, SC)
        gated = [gated0, gated1]
        prod, pos, xg = cut(late, [NT * TOPK * E, NT * E, UNROLL * D])
        pos, xg = chunks(pos, NT), chunks(xg, UNROLL)
        ring = cut(late, [UNROLL * D, C * P, C * P, P, P, P, P])
        yo, xT, gate, hidden = chunks(ring[0], UNROLL), [chunks(r, C) for r in ring[1:3]], ring[3:5], ring[5:7]
        hiddenT = [sb(f"hiddenT{i}", [P, EH]) for i in range(2)]
        meta, mine, mtmp = (chunks(m, SLOT_TILES)
                            for m in cut(early, [SLOT_TILES * META, SLOT_TILES * TOPK, SLOT_TILES * TOPK]))
        zring = [chunks(z, TOPK) for z in cut(early, [TOPK * D] * 4)]
        zsum = [chunks(z, 2) for z in cut(early, [TOPK * D] * 4 + [2 * D] * 2)[4:]]

        bk_s = sb("bk_s", [P, C])
        bq_s = sb("bq_s", [P, C])
        bc_s = sb("bc_s", [P, D])
        rw_s = sb("rw_s", [P, C, E])
        rb_s = sb("rb_s", [P, E])
        ident = sb("ident", [P, P])
        identb = sb("identb", [P, P], BF16)
        stats = sb("stats", [P, QT, 6])
        mv = sb("mv", [P, QT, 2])
        rstd = sb("rstd", [P, QT])
        minus_half = sb("minus_half", [P, QT])
        mx = sb("mx", [P, 2, UNITS])
        mres = sb("mres", [P, UNITS])
        msplit = sb("msplit", [P, QT, 3, GH], BF16)
        mrow = sb("mrow", [3 * GH, T], BF16)
        den = sb("den", [P, QT, GH])
        logits = sb("logits", [P, NT, E])
        top = sb("top", [P, NT, 8])
        top_i = sb("top_i", [P, NT, 8], U32)
        top_f = sb("top_f", [P, NT, TOPK])
        rstat = sb("rstat", [P, NT])
        onehot = sb("onehot", [P, NT, TOPK, E], BF16)
        mask = sb("mask", [P, NT, E], BF16)
        zeros = sb("zeros", [P, ROW])
        iota_i = sb("iota_i", [P, SLOT_TILES], I32)
        iota_e = sb("iota_e", [P, E])
        iota_p = sb("iota_p", [P, 1])
        iota_j = sb("iota_j", [P, TOPK])
        my_slot = sb("my_slot", [P, SLOT_TILES])
        dummy = sb("dummy_row", [P, SLOT_TILES])
        before = sb("before", [P, P], BF16)
        upto = sb("upto", [E, 2, E], BF16)
        onesb = sb("onesb", [P, P], BF16)
        cnt_i = sb("cnt_i", [E, 1], I32)
        tiles_b = sb("tiles_b", [E, P], BF16)
        base = sb("base", [P, E])
        tile_cmp = sb("tile_cmp", [P, E])
        tile_e = sb("tile_e", [P, 1])
        tile_eb = sb("tile_eb", [P, 1], BF16)
        offs = sb("offs", [1, SLOT_TILES], I32)
        slot_f = sb("slot_f", [P, NT * TOPK])
        slot_i = sb("slot_i", [P, NT * TOPK], I32)
        wgt = sb("wgt", [P, SLOT_TILES])
        found = sb("found", [P, SLOT_TILES])
        dest_f = sb("dest_f", [P, SLOT_TILES])
        dest = sb("dest", [P, SLOT_TILES], I32)
        dest_k = [sb(f"dest_k{i}", [P, 1], I32) for i in range(UNROLL)]

        s_bank = [ps(f"s_bank{i}", [P, T]) for i in range(S_BANKS)]
        m_bank = [ps(f"m_bank{i}", [P, T]) for i in range(M_BANKS)]
        o_bank = [ps(f"o_bank{i}", [P, T]) for i in range(2)]
        misc = ps("misc", [P, T])
        miscb = misc[:, :].bitcast(BF16)

        ld_x = [sem(f"ld_x{b}") for b in range(B)]
        ld_cT = sem("ld_cT")
        ld_cn = sem("ld_cn")
        ld_wk = sem("ld_wk")
        ld_wq = sem("ld_wq")
        ld_b = sem("ld_b")
        ld_wc = sem("ld_wc")
        idents = sem("idents")
        init = sem("init")
        norm1 = sem("norm1")
        misc_full = sem("misc_full")
        misc_free = sem("misc_free")
        full_rdy = sem("full_rdy")
        split = sem("split")
        parts_out = [sem(f"parts_out{i}") for i in range(2)]
        opnd = [sem(f"opnd{i}") for i in range(2)]
        v_rdy = sem("v_rdy")
        m_full = sem("m_full")
        m_done = sem("m_done")
        msp = sem("msp")
        shift = [sem(f"shift{i}") for i in range(2)]
        s_full = sem("s_full")
        exp_done = sem("exp_done")
        pv_done = sem("pv_done")
        o_rdy = sem("o_rdy")
        norm2 = sem("norm2")
        resid = sem("resid")
        var1 = sem("var1")
        pow_done = sem("pow_done")
        dchain = sem("dchain")
        pchain = sem("pchain")
        stored = sem("stored")
        filled = sem("filled")
        ld_sh = sem("ld_sh")
        ld_w = sem("ld_w")
        zero_rdy = sem("zero_rdy")
        consts = sem("consts")
        r_sub = sem("r_sub")
        r_exp = sem("r_exp")
        mask_rdy = sem("mask_rdy")
        ranks = sem("ranks")
        tiles_rdy = sem("tiles_rdy")
        bases = sem("bases")
        tile_e_rdy = sem("tile_e_rdy")
        tile_row = sem("tile_row")
        offs_rdy = sem("offs_rdy")
        slots_rdy = sem("slots_rdy")
        scattered = sem("scattered")
        ld_meta = sem("ld_meta")
        dest_rdy = sem("dest_rdy")
        sg_full = sem("sg_full")
        sg_act = sem("sg_act")
        sg_hid = sem("sg_hid")
        sd_full = sem("sd_full")
        sd_out = sem("sd_out")
        ld_xg = [sem(f"ld_xg{i}") for i in range(UNROLL)]
        x_full = sem("x_full")
        x_rdy = sem("x_rdy")
        g_full = sem("g_full")
        g_act = sem("g_act")
        h_rdy = sem("h_rdy")
        ht_full = sem("ht_full")
        ht_rdy = sem("ht_rdy")
        y_full = sem("y_full")
        yo_rdy = sem("yo_rdy")
        dest_cp = sem("dest_cp")
        z_out = [sem(f"z_out{i}") for i in range(UNROLL)]
        ld_z = [sem(f"ld_z{i}") for i in range(4)]
        z_sum = sem("z_sum")

        block = ctx.enter_context(nc.Block())

        def slots():
            return range(FIRST_SLOT, LAST_SLOT + 1)

        def projection_no(b, name, c):
            return 4 * b + 2 * (name == "Q") + c

        @block.sync
        def _(sp):
            def load_ctx(b):
                if b:
                    sp.wait_ge(misc_full, through("K", b - 1, 1))
                sp.dma_start(cT[:, :, :], ctxT[:, b * T:(b + 1) * T].rearrange("(c p) t -> p c t", p=P)).then_inc(ld_cT, 16)

            def load_values(b):
                if b:
                    sp.wait_ge(v_rdy, b)
                sp.dma_start(cn[:, :, :], ctxn[b * T:(b + 1) * T, :].rearrange("(k p) d -> p k d", p=P)).then_inc(ld_cn, 16)

            def load_x(b):
                sp.dma_start(xres[:, b * QT:(b + 1) * QT, :],
                             x[b * T:(b + 1) * T, :].rearrange("(k p) d -> p k d", p=P)).then_inc(ld_x[b], 16)

            sp.dma_start(wk[:, :, :], wkT.rearrange("(c p) n -> p c n", p=P)).then_inc(ld_wk, 16)
            load_ctx(0)
            load_values(0)
            load_x(0)
            sp.dma_start(bk_s[:, :], bk).then_inc(ld_b, 16)
            sp.dma_start(bq_s[:, :], bq).then_inc(ld_b, 16)
            sp.dma_start(wq[:, :, :], wqT.rearrange("(c p) n -> p c n", p=P)).then_inc(ld_wq, 16)
            load_x(1)
            load_x(2)
            load_x(3)
            sp.dma_start(wc[:, :, :], wcT.rearrange("(c p) n -> p c n", p=P)).then_inc(ld_wc, 16)
            sp.dma_start(bc_s[:, :], bc).then_inc(ld_wc, 16)
            sp.dma_start(rw_s[:, :, :], rwT.rearrange("(c p) n -> p c n", p=P)).then_inc(ld_wc, 16)
            sp.dma_start(rb_s[:, :], rb).then_inc(ld_wc, 16)

            def store_parts(b, name, c):
                n = projection_no(b, name, c)
                sp.wait_ge(split, n + 1)
                sp.dma_start(parts_d[b, int(name == "Q"), :, c * P:(c + 1) * P, :].rearrange("s p t -> p s t"),
                             part[n % 2][:, :, :]).then_inc(parts_out[n % 2], 16)

            def stack(b, name):
                n = projection_no(b, name, 1)
                sp.wait_ge(parts_out[0], 8 * (n + 1))
                sp.wait_ge(parts_out[1], 8 * (n + 1))
                if b >= 2:
                    sp.wait_ge(s_full, UNITS * BG * (b - 1))
                dst, which = (qs[b % 2], Q_PART) if name == "Q" else (ks[b % 2], K_PART)
                for i, s in enumerate(which):
                    sp.dma_start(dst[i * HD:(i + 1) * HD, :, :],
                                 parts_d[b, int(name == "Q"), s].rearrange("(h d) t -> d h t", d=HD)).then_inc(opnd[b % 2], 16)

            def shift_rows(g):
                b, gg = divmod(g, BG)
                sp.wait_ge(misc_free, through("MR", g))
                for s in range(3):
                    sp.dma_start(qs[b % 2][SHIFT_ROW + s:SHIFT_ROW + s + 1, gg * GH:(gg + 1) * GH, :],
                                 mrow[s * GH:(s + 1) * GH, :]).then_inc(shift[g % 2], 16)

            for s in slots():
                for name, *arg in STAGES_AT.get(s, ()):
                    if name in ("K", "Q"):
                        b, c = arg
                        store_parts(b, name, c)
                        if (name, c) == ("K", 1) and b + 1 < B:
                            load_ctx(b + 1)
                        if c == 1 and b < 2:
                            stack(b, name)
                            if name == "K":
                                load_values(b + 1)
                    if name == "MR":
                        shift_rows(*arg)
                if s == UNITS * BG + 12:
                    load_values(3)
                if s >= 10 and (s - 10) % 20 == 0 and (s - 10) // 20 < FILLS:
                    i = (s - 10) // 20
                    if i == 0:
                        sp.wait_ge(zero_rdy, 1)
                    sp.dma_start(slot_rows[i * FILL_TILES * P:(i + 1) * FILL_TILES * P, :].rearrange("(t p) r -> p t r", p=P),
                                 zeros[:, :].unsqueeze(1).to_broadcast([P, FILL_TILES, ROW])).then_inc(filled, 16)
                if s == UNITS * BG * (B - 2) + 20:
                    sp.wait_ge(misc_full, through("Q", B - 1, 1))
                    sp.wait_ge(v_rdy, B)
                    sp.wait_ge(split, 4 * B)
                    for i in range(2):
                        sp.wait_ge(parts_out[i], 16 * 2 * B)
                    sp.dma_start(sg, sgT.rearrange("(c p) n -> p c n", p=P)).then_inc(ld_sh, 16)
                    sp.dma_start(su, suT.rearrange("(c p) n -> p c n", p=P)).then_inc(ld_sh, 16)
                    sp.dma_start(sd, sdT.rearrange("(c p) n -> p c n", p=P)).then_inc(ld_sh, 16)
                if s == ALL:
                    sp.wait_ge(pv_done, ALL)
                    q = E * WORDS // 4
                    for i in range(4):
                        sp.dma_start(weights[:, i * q:(i + 1) * q], wall[:, i * q:(i + 1) * q]).then_inc(ld_w, 16)
                if s >= 0 and s % (UNITS * BG) == 0 and 2 <= s // (UNITS * BG) + 1 < B:
                    stack(s // (UNITS * BG) + 1, "K")
                    stack(s // (UNITS * BG) + 1, "Q")

            sp.wait_ge(scattered, 16 * NT * TOPK)

            def load_rows(k, r):
                if not isinstance(k, int) or k >= UNROLL:
                    sp.wait_ge(x_full, k - UNROLL + 1)
                sp.dma_start(xg[:, r, :], slot_rows[bass.ds(k * P, P), 0:D]).then_inc(ld_xg[r], 16)

            for k in range(UNROLL):
                load_rows(k, k)
            sp.wait_ge(sd_out, 2 * B)
            sp.dma_start(meta[:, :, :], slot_rows[:, D:ROW].rearrange("(t p) m -> p t m", p=P)).then_inc(ld_meta, 16)
            with sp.Fori(1, SLOT_TILES // UNROLL) as i:
                for r in range(UNROLL):
                    load_rows(i * UNROLL + r, r)

            for i in range(UNROLL):
                sp.wait_ge(z_out[i], 16 * (SLOT_TILES // UNROLL))
            for t in range(NT):
                if t >= 4:
                    sp.wait_ge(z_sum, t - 3)
                sp.dma_start(zring[t % 4], choice_rows[t * P * TOPK:(t + 1) * P * TOPK, :].rearrange("(p j) d -> p j d", j=TOPK))\
                    .then_inc(ld_z[t % 4], 16)

        @block.tensor
        def _(pe):
            def stage(name, *arg):
                no = STAGE_NO[(name, *arg)]
                if no:
                    pe.wait_ge(misc_free, no)
                if name in ("K", "Q"):
                    b, c = arg
                    if name == "K":
                        pe.wait_ge(ld_cT, 16 * (b + 1))
                        pe.wait_ge(ld_wk, 16)
                    else:
                        pe.wait_ge(misc_free, through("NT", b, 1))
                        pe.wait_ge(ld_wq, 16)
                    w, act = (wk, cT) if name == "K" else (wq, xnT)
                    for i in range(C):
                        mm = pe.matmul(misc[:, :], w[:, i, c * P:(c + 1) * P], act[:, i, :], start=i == 0, stop=i == C - 1)
                elif name == "NT":
                    b, c = arg
                    pe.wait_ge(norm1, b + 1)
                    pe.wait_ge(idents, 1)
                    for t in range(QT):
                        mm = pe.transpose(misc[:, t * P:(t + 1) * P], xrow[:, b * QT + t, c * P:(c + 1) * P], ident[:, :])
                elif name == "MR":
                    pe.wait_ge(msp, arg[0] + 1)
                    pe.wait_ge(idents, 2)
                    for t in range(QT):
                        mm = pe.transpose(miscb[0:3 * GH, t * P:(t + 1) * P], msplit[:, t, :, :].rearrange("p s j -> p (s j)"), identb[:, :])
                elif name == "YT":
                    pe.wait_ge(o_rdy, arg[0] + 1)
                    for t in range(QT):
                        mm = pe.transpose(misc[:, t * P:(t + 1) * P], o_sb[:, t * P:(t + 1) * P], ident[:, :])
                elif name == "AT":
                    b, c = arg
                    pe.wait_ge(misc_free, through("YT", BG * b + BG - 1))
                    for t in range(QT):
                        mm = pe.transpose(misc[:, t * P:(t + 1) * P], y[:, t, c * P:(c + 1) * P], ident[:, :])
                elif name == "WC":
                    b, half = arg
                    pe.wait_ge(misc_free, through("AT", b, 1))
                    pe.wait_ge(ld_wc, 64)
                    for t in range(2):
                        for i in range(C):
                            k = (2 * half + t) * P
                            mm = pe.matmul(misc[:, t * D:(t + 1) * D], yT[:, i, k:k + P], wc[:, i, :],
                                           start=i == 0, stop=i == C - 1)
                elif name == "XT":
                    b, c = arg
                    pe.wait_ge(norm2, b + 1)
                    for t in range(QT):
                        mm = pe.transpose(misc[:, t * P:(t + 1) * P], xrow[:, b * QT + t, c * P:(c + 1) * P], ident[:, :])
                elif name == "LG":
                    b = arg[0]
                    pe.wait_ge(misc_free, through("XT", b, 1))
                    for t in range(QT):
                        for i in range(C):
                            k = (b * QT + t) * P
                            mm = pe.matmul(misc[:, t * E:(t + 1) * E], xn2T[:, i, k:k + P], rw_s[:, i, :],
                                           start=i == 0, stop=i == C - 1)
                mm.then_inc(misc_full, 1)

            for s in slots():
                if 0 <= s < ALL:
                    g, b, h, t, j = unit(s)
                    if s == 0:
                        pe.wait_ge(init, 2)
                    if s % UNITS == 0:
                        pe.wait_ge(shift[g % 2], 48 * (g // 2 + 1))
                    if s >= S_BANKS:
                        pe.wait_ge(exp_done, s - S_BANKS + 1)
                    pe.matmul(s_bank[s % S_BANKS][:, :], ks[b % 2][0:ROWS, h, t * P:(t + 1) * P], qs[b % 2][0:ROWS, h, :],
                              start=True, stop=True).then_inc(s_full, 1)
                n = s + AHEAD
                if 0 <= n < ALL:
                    g, b, h, t, j = unit(n)
                    if n % (UNITS * BG) == 0:
                        pe.wait_ge(opnd[b % 2], 16 * 2 * BLOCKS * (b // 2 + 1))
                    if n >= M_BANKS:
                        pe.wait_ge(m_done, n - M_BANKS + 1)
                    pe.matmul(m_bank[n % M_BANKS][:, :], qs[b % 2][0:SHIFT_ROW, h, t * P:(t + 1) * P],
                              ks[b % 2][0:SHIFT_ROW, h, :], start=True, stop=True).then_inc(m_full, 1)
                n = s - LAG
                if 0 <= n < ALL:
                    g, b, h, t, j = unit(n)
                    if n % (UNITS * BG) == 0:
                        pe.wait_ge(v_rdy, b + 1)
                    if n % UNITS == 0 and g >= 2:
                        pe.wait_ge(o_rdy, g - 1)
                    pe.wait_ge(exp_done, n + 1)
                    pe.matmul(o_bank[g % 2][32 * j:32 * (j + 1), :], vaug[b % 2][:, t, h, :], expo[n % P_RING],
                              start=t == 0, stop=t == QT - 1).then_inc(pv_done, 1)
                for st in STAGES_AT.get(s, ()):
                    stage(*st)

            pe.wait_ge(misc_free, through("LG", B - 1, 0))
            pe.wait_ge(mask_rdy, B)
            pe.wait_ge(consts, 1)
            m2 = mask[:, :, :].rearrange("p t e -> p (t e)")
            pe.matmul(misc[:, :], before[:, :], m2, start=True, stop=False)
            for t in range(1, NT):
                pe.matmul(misc[:, t * E:], onesb[:, :], m2[:, 0:(NT - t) * E], start=False, stop=t == NT - 1)
            pe.wait_ge(exp_done, ALL)
            small = s_bank[2]
            for t in range(NT):
                mm = pe.matmul(small[0:E, 0:1], mask[:, t, :], onesb[:, 0:1], start=t == 0, stop=t == NT - 1)
            mm.then_inc(ranks, 1)

            def shared_up(k):
                b, c = divmod(k, SC)
                if k >= 2:
                    pe.wait_ge(sg_hid, k - 1)
                for w, bank in ((sg, s_bank[k % 2]), (su, m_bank[k % 2])):
                    for i in range(C):
                        mm = pe.matmul(bank[:, :], w[:, i, c * P:(c + 1) * P], xn2T[:, i, b * T:(b + 1) * T],
                                       start=i == 0, stop=i == C - 1)
                mm.then_inc(sg_full, 1)

            def shared_down(k):
                b, c = divmod(k, SC)
                pe.wait_ge(sg_hid, k + 1)
                if c == 0 and b:
                    pe.wait_ge(sd_out, 2 * b)
                for t in range(QT):
                    mm = pe.matmul(o_bank[t // 2][:, t % 2 * D:(t % 2 + 1) * D], hid[:, c, t * P:(t + 1) * P], sd[:, c, :],
                                   start=c == 0 and t % 2 == 0, stop=c == SC - 1, skip_group_check=True)
                mm.then_inc(sd_full, 1)

            pe.wait_ge(ld_sh, 48)
            pe.wait_ge(m_done, ALL)
            pe.wait_ge(o_rdy, GROUPS)
            for k in range(B * SC):
                shared_up(k)
                if k == 0:
                    pe.wait_ge(tiles_rdy, 1)
                    pe.matmul(small[:, 64:64 + 2 * E], tiles_b[:, :], upto[:, :, :].rearrange("p a b -> p (a b)"),
                              start=True, stop=True).then_inc(bases, 1)
                if k == 1:
                    pe.wait_ge(tile_e_rdy, 1)
                    pe.matmul(small[0:1, 256:256 + SLOT_TILES], tile_eb[0:SLOT_TILES, 0:1], identb[0:SLOT_TILES, 0:SLOT_TILES],
                              start=True, stop=True).then_inc(tile_row, 1)
                if k:
                    shared_down(k - 1)
            shared_down(B * SC - 1)

            pe.wait_ge(sd_out, 2 * B)
            pe.wait_ge(offs_rdy, 1)
            pe.wait_ge(slots_rdy, 1)
            pe.wait_ge(ld_w, 64)
            y_bank = [s_bank[2], misc]

            def step(k, r):
                fixed = isinstance(k, int)
                if not fixed or 3 <= k <= SLOT_TILES + 2:
                    w3 = pe.value_load(offs[0:1, bass.ds(k - 3, 1)], min_val=0, max_val=(E - 1) * WORDS)
                if not fixed or 1 <= k <= SLOT_TILES:
                    w1 = pe.value_load(offs[0:1, bass.ds(k - 1, 1)], min_val=0, max_val=(E - 1) * WORDS)
                if not fixed or k < SLOT_TILES:
                    pe.wait_ge(ld_xg[r], 16 * (k // UNROLL + 1) if fixed else (k - r) * (16 // UNROLL) + 16)
                    for i in range(C):
                        mm = pe.transpose(s_bank[r % 2][:, i * P:(i + 1) * P], xg[:, r, i * P:(i + 1) * P], ident[:, :])
                    mm.then_inc(x_full, 1)
                if not fixed or 1 <= k <= SLOT_TILES:
                    q = (r - 1) % 2
                    pe.wait_ge(x_rdy, k)
                    for i in range(C):
                        mm = pe.matmul(m_bank[q][:, 0:2 * EH], xT[q][:, i, :], weights[:, bass.ds(w1 + i * D, 2 * EH)],
                                       start=i == 0, stop=i == C - 1)
                    mm.then_inc(g_full, 1)
                if not fixed or 2 <= k <= SLOT_TILES + 1:
                    q = (r - 2) % 2
                    pe.wait_ge(h_rdy, k - 1)
                    pe.transpose(o_bank[q][:, 0:P], hidden[q], ident[:, :]).then_inc(ht_full, 1)
                if not fixed or 3 <= k <= SLOT_TILES + 2:
                    q = (r - 3) % 2
                    pe.wait_ge(ht_rdy, k - 2)
                    if not fixed or k >= 5:
                        pe.wait_ge(yo_rdy, k - 4)
                    pe.matmul(y_bank[q][:, 0:D], hiddenT[q][:, :], weights[:, bass.ds(w3 + C * D, D)],
                              start=True, stop=True).then_inc(y_full, 1)

            for k in range(UNROLL):
                step(k, k)
            with pe.Fori(1, SLOT_TILES // UNROLL) as i:
                for r in range(UNROLL):
                    step(i * UNROLL + r, r)
            for k in range(SLOT_TILES, SLOT_TILES + DEPTH):
                step(k, k % UNROLL)

        @block.scalar
        def _(act):
            def stage(name, *arg):
                if name in ("K", "Q"):
                    b, c = arg
                    n = projection_no(b, name, c)
                    act.wait_ge(misc_full, through(name, *arg))
                    if n == 0:
                        act.wait_ge(ld_b, 32)
                    if n >= 2:
                        act.wait_ge(split, n - 1)
                        act.wait_ge(parts_out[n % 2], 16 * (n // 2))
                    bias = (bk_s if name == "K" else bq_s)[:, c:c + 1]
                    act.activation(full[n % 2][:, :], misc[:, :], ACT.Identity, bias=bias).then_inc(full_rdy, 1)
                    act.activation(part[n % 2][:, 0, :], misc[:, :], ACT.Identity, bias=bias).then_inc(misc_free, 1)
                elif name == "NT":
                    b, c = arg
                    act.wait_ge(misc_full, through(name, *arg))
                    act.copy(xnT[:, c, :], misc[:, :]).then_inc(misc_free, 1)
                elif name == "AT":
                    b, c = arg
                    act.wait_ge(misc_full, through(name, *arg))
                    act.copy(yT[:, c, :], misc[:, :]).then_inc(misc_free, 1)
                elif name == "XT":
                    b, c = arg
                    act.wait_ge(misc_full, through(name, *arg))
                    act.copy(xn2T[:, c, b * T:(b + 1) * T], misc[:, :]).then_inc(misc_free, 1)

            for s in slots():
                if 0 <= s < ALL:
                    act.wait_ge(s_full, s + 1)
                    if s >= P_RING:
                        act.wait_ge(pv_done, s - P_RING + 1)
                    act.activation(expo[s % P_RING], s_bank[s % S_BANKS][:, :], ACT.Exp, scale=SCALE).then_inc(exp_done, 1)
                g, u = divmod(s - LAG, UNITS)
                g -= 1
                if u == 0 and 0 <= g < GROUPS:
                    act.wait_ge(pv_done, UNITS * (g + 1))
                    if g:
                        act.wait_ge(misc_full, through("YT", g - 1))
                    act.copy(o_sb[:, :], o_bank[g % 2][:, :]).then_inc(o_rdy, 1)
                for st in STAGES_AT.get(s - 1, ()):
                    stage(*st)
                for b, slot in ROUTE_SLOT.items():
                    if s == slot + 2:
                        act.wait_ge(r_sub, b + 1)
                        lg = logits[:, b * QT:(b + 1) * QT, :]
                        act.activation(lg, lg, ACT.Exp).then_inc(r_exp, 1)

            for k in range(B * SC):
                act.wait_ge(sg_full, k + 1)
                if k >= 2:
                    act.wait_ge(sg_hid, k - 1)
                act.activation(gated[k % 2], s_bank[k % 2][:, :], ACT.Silu).then_inc(sg_act, 1)

            def step(k, r):
                fixed = isinstance(k, int)
                if not fixed or 1 <= k <= SLOT_TILES:
                    q = (r - 1) % 2
                    act.wait_ge(g_full, k)
                    act.activation(gate[q], m_bank[q][:, 0:EH], ACT.Silu).then_inc(g_act, 1)
                if not fixed or 2 <= k <= SLOT_TILES + 1:
                    q = (r - 2) % 2
                    act.wait_ge(ht_full, k - 1)
                    act.copy(hiddenT[q][:, :], o_bank[q][:, 0:P]).then_inc(ht_rdy, 1)
                if not fixed or 3 <= k <= SLOT_TILES + 2:
                    q, o = (r - 3) % 2, (r - 3) % UNROLL
                    if fixed and k == 3:
                        act.wait_ge(dest_rdy, 1)
                    act.wait_ge(y_full, k - 2)
                    if not fixed:
                        act.wait_ge(z_out[o], (k - r) * (16 // UNROLL) - (16 if r < DEPTH else 0))
                    elif k - 3 >= UNROLL:
                        act.wait_ge(z_out[o], 16 * ((k - 3) // UNROLL))
                    act.activation(yo[:, o, :], [s_bank[2], misc][q][:, 0:D], ACT.Copy,
                                   scale=wgt[:, bass.ds(k - 3, 1)]).then_inc(yo_rdy, 1)

            for k in range(2 * UNROLL):
                step(k, k % UNROLL)
            with act.Fori(2, SLOT_TILES // UNROLL) as i:
                for r in range(UNROLL):
                    step(i * UNROLL + r, r)
            for k in range(SLOT_TILES, SLOT_TILES + DEPTH):
                step(k, k % UNROLL)

            for t in range(NT):
                act.wait_ge(z_sum, t + 1)
                act.dma_start(out[t * P:(t + 1) * P, :], xres[:, t, :]).then_inc(stored, 16)
            act.wait_ge(stored, 16 * NT)

        @block.gpsimd
        def _(pool):
            chain = [0]

            def link(ins):
                chain[0] += 1
                ins.then_inc(pchain, 1)
                pool.wait_ge(pchain, chain[0])

            link(pool.memset(ident[:, :], 0.0))
            link(pool.affine_select(out=ident[:, :], in_=ident[:, :], compare_op=ALU.not_equal, fill=1.0, base=0,
                                    pattern=[[-1, P]], channel_multiplier=1))
            pool.tensor_copy(identb[:, :], ident[:, :]).then_inc(idents, 2)
            link(pool.memset(minus_half[:, :], -0.5))
            link(pool.memset(zeros[:, :], 0.0))
            pool.nop().then_inc(zero_rdy, 1)
            for i in range(2):
                link(pool.memset(vaug[i], 0.0))
                link(pool.memset(vaug[i][:, :, :, HD:HD + 1], 1.0))

            def values(b):
                pool.wait_ge(ld_cn, 16 * (b + 1))
                if b >= 2:
                    pool.wait_ge(pv_done, UNITS * BG * (b - 1))
                pool.tensor_copy(vaug[b % 2].rearrange("p k h m -> p (k h) m")[:, :, 0:HD],
                                 cn[:, :, :].rearrange("p k (h d) -> p (k h) d", h=H)).then_inc(v_rdy, 1)

            def split_projection(b, name, c):
                n = projection_no(b, name, c)
                pool.wait_ge(misc_free, through(name, b, c))
                pool.wait_ge(full_rdy, n + 1)
                if n:
                    pool.wait_ge(split, n)
                f, p = full[n % 2], part[n % 2]
                link(pool.tensor_tensor(rest[:, :], f[:, :], p[:, 0, :], ALU.subtract))
                link(pool.tensor_copy(p[:, 1, :], rest[:, :]))
                pool.tensor_tensor(p[:, 2, :], rest[:, :], p[:, 1, :], ALU.subtract).then_inc(split, 1)

            def split_maxima(g):
                pool.wait_ge(m_done, UNITS * (g + 1))
                if g:
                    pool.wait_ge(misc_full, through("MR", g - 1))
                    pool.wait_ge(msp, g)
                m = mx[:, g % 2, :].rearrange("p (t j) -> p t j", t=QT)
                r = mres[:, :].rearrange("p (t j) -> p t j", t=QT)
                link(pool.tensor_copy(msplit[:, :, 0, :], m))
                link(pool.tensor_tensor(r, m, msplit[:, :, 0, :], ALU.subtract))
                link(pool.tensor_copy(msplit[:, :, 1, :], r))
                pool.tensor_tensor(msplit[:, :, 2, :], r, msplit[:, :, 1, :], ALU.subtract).then_inc(msp, 1)

            def constants():
                def indices(out, pattern, base, step):
                    n = out.shape[1]
                    i = iota_i[0:out.shape[0], 0:n]
                    link(pool.iota(i, pattern, base=base, channel_multiplier=step))
                    link(pool.tensor_copy(out, i))

                indices(iota_e[:, :], [[1, E]], 0, 0)
                indices(iota_p[:, :], [[1, 1]], 0, 1)
                indices(iota_j[:, :], [[1, TOPK]], 0, 0)
                indices(my_slot[:, :], [[P, SLOT_TILES]], 1, 1)
                indices(dummy[:, :], [[P, SLOT_TILES]], N * TOPK, 1)
                indices(top_f[:, :, 0], [[P, NT]], 0, 1)
                link(pool.memset(onesb[:, :], 1.0))
                link(pool.affine_select(out=before[:, :], in_=onesb[:, :], compare_op=ALU.is_gt, fill=0.0, base=0,
                                        pattern=[[1, P]], channel_multiplier=-1))
                link(pool.affine_select(out=upto[:, 0, :], in_=onesb[0:E, 0:E], compare_op=ALU.is_gt, fill=0.0, base=0,
                                        pattern=[[1, E]], channel_multiplier=-1))
                link(pool.affine_select(out=upto[:, 1, :], in_=onesb[0:E, 0:E], compare_op=ALU.is_ge, fill=0.0, base=0,
                                        pattern=[[1, E]], channel_multiplier=-1))
                pool.tensor_copy(xrow[:, :, M_TOKEN], top_f[:, :, 0]).then_inc(consts, 1)

            for s in slots():
                if s == 2:
                    constants()
                for (which, b), slot in NORM_SLOTS.items():
                    if s == slot:
                        no = NORM_NO[(which, b)]
                        pool.wait_ge(var1, no + 1)
                        link(pool.tensor_scalar(rstd[:, :], mv[:, :, 1], LN_EPS, None, ALU.add))
                        pool.tensor_tensor(rstd[:, :], rstd[:, :], minus_half[:, :], ALU.pow).then_inc(pow_done, 1)
                    if s == slot + NORM_GAP + 1 and which == 1:
                        pool.wait_ge(norm1, b + 1)
                        if b == 0:
                            pool.wait_ge(ld_wc, 64)
                        r = xres[:, b * QT:(b + 1) * QT, :]
                        pool.tensor_tensor(r, r, bc_s[:, :].rearrange("p (o n) -> p o n", o=1).to_broadcast([P, QT, D]), ALU.add)\
                            .then_inc(resid, 1)
                for name, *arg in STAGES_AT.get(s, ()):
                    if name in ("K", "Q"):
                        split_projection(arg[0], name, arg[1])
                    if (name, *arg) == ("K", 0, 1):
                        values(0)
                    if (name, *arg) == ("K", 1, 1):
                        values(1)
                g, u = divmod(s + AHEAD, UNITS)
                if u == 0 and 1 <= g <= GROUPS:
                    split_maxima(g - 1)
                b, u = divmod(s, UNITS * BG)
                if u == LAG + 4 and b >= 1 and b + 1 < B:
                    values(b + 1)

            pool.wait_ge(slots_rdy, 1)
            pool.wait_ge(filled, 16 * FILLS)
            for t in range(NT):
                for j in range(TOPK):
                    n = t * TOPK + j
                    pool.indirect_dma_start(slot_rows, bass.IndirectOffsetOnAxis(ap=slot_i[:, n:n + 1], axis=0),
                                            xrow[:, t, :], None).then_inc(scattered, 16)
            pool.wait_ge(dest_rdy, 1)

            def fetch_destinations(k, r):
                if not isinstance(k, int) or k >= UNROLL:
                    pool.wait_ge(z_out[r], k // UNROLL * 16 if isinstance(k, int) else (k - r) * (16 // UNROLL))
                pool.tensor_copy(dest_k[r][:, :], dest[:, bass.ds(k, 1)]).then_inc(dest_cp, 1)

            def scatter(k, r):
                pool.wait_ge(yo_rdy, k + 1)
                pool.wait_ge(dest_cp, k + 1)
                if not isinstance(k, int) or k + 1 < SLOT_TILES:
                    fetch_destinations(k + 1, (r + 1) % UNROLL)
                pool.indirect_dma_start(choice_rows, bass.IndirectOffsetOnAxis(ap=dest_k[r][:, 0:1], axis=0),
                                        yo[:, r, :], None).then_inc(z_out[r], 16)

            fetch_destinations(0, 0)
            for k in range(UNROLL):
                scatter(k, k)
            with pool.Fori(1, SLOT_TILES // UNROLL - 1) as i:
                for r in range(UNROLL):
                    scatter(i * UNROLL + r, r)
            for k in range(SLOT_TILES - UNROLL, SLOT_TILES):
                scatter(k, k % UNROLL)

        @block.vector
        def _(dve):
            chain = [0]

            def link(ins):
                chain[0] += 1
                ins.then_inc(dchain, 1)
                dve.wait_ge(dchain, chain[0])

            for i in range(2):
                dve.memset(ks[i][SHIFT_ROW:ROWS, :, :], 1.0).then_inc(init, 1)

            def norm_statistics(which, b):
                no = NORM_NO[(which, b)]
                if which == 1:
                    dve.wait_ge(ld_x[b], 16)
                else:
                    dve.wait_ge(misc_free, through("WC", b, 1))
                for t in range(QT):
                    last = dve.bn_stats(stats[:, t, :], xres[:, b * QT + t, :])
                link(last)
                for t in range(QT):
                    last = dve.bn_aggr(mv[:, t, :], stats[:, t, :])
                last.then_inc(var1, 1)

            def norm_scaling(which, b):
                no = NORM_NO[(which, b)]
                dve.wait_ge(pow_done, no + 1)
                if which == 2:
                    dve.wait_ge(misc_full, through("NT", b, 1))
                for t in range(QT):
                    last = dve.tensor_scalar(xrow[:, b * QT + t, 0:D], xres[:, b * QT + t, :], mv[:, t, 0:1],
                                             rstd[:, t:t + 1], ALU.subtract, ALU.mult)
                last.then_inc(norm1 if which == 1 else norm2, 1)

            def stage(name, *arg):
                if name == "MR":
                    g, = arg
                    dve.wait_ge(misc_full, through(name, *arg))
                    if g:
                        dve.wait_ge(shift[(g - 1) % 2], 48 * ((g - 1) // 2 + 1))
                    dve.tensor_copy(mrow[:, :], miscb[0:3 * GH, 0:T]).then_inc(misc_free, 1)
                elif name == "YT":
                    g, = arg
                    dve.wait_ge(misc_full, through(name, *arg))
                    o = misc[:, :].rearrange("p (t j m) -> p t j m", t=QT, j=GH)
                    link(dve.reciprocal(den[:, :, :], o[:, :, :, HD]))
                    gg = g % BG
                    dve.tensor_tensor(y[:, :, gg * GH * HD:(gg + 1) * GH * HD].rearrange("p t (j d) -> p t j d", j=GH),
                                      o[:, :, :, 0:HD], den[:, :, :].unsqueeze(3).to_broadcast([P, QT, GH, HD]), ALU.mult)\
                        .then_inc(misc_free, 1)
                elif name == "WC":
                    b, half = arg
                    dve.wait_ge(misc_full, through(name, *arg))
                    dve.wait_ge(resid, b + 1)
                    r = xres[:, b * QT + 2 * half:b * QT + 2 * half + 2, :]
                    dve.tensor_tensor(r, misc[:, :].rearrange("p (t n) -> p t n", t=2), r, ALU.add).then_inc(misc_free, 1)
                elif name == "LG":
                    b = arg[0]
                    dve.wait_ge(misc_full, through(name, *arg))
                    dve.tensor_tensor(logits[:, b * QT:(b + 1) * QT, :], misc[:, 0:QT * E].rearrange("p (t e) -> p t e", t=QT),
                                      rb_s[:, :].unsqueeze(1).to_broadcast([P, QT, E]), ALU.add).then_inc(misc_free, 1)

            def route_sub(b):
                dve.wait_ge(misc_free, through("LG", b, 0))
                lg, st = logits[:, b * QT:(b + 1) * QT, :], rstat[:, b * QT:(b + 1) * QT]
                link(dve.tensor_reduce(st, lg, AX.X, ALU.max))
                dve.tensor_tensor(lg, lg, st.unsqueeze(2).to_broadcast([P, QT, E]), ALU.subtract).then_inc(r_sub, 1)

            def route(b):
                tiles = slice(b * QT, (b + 1) * QT)
                lg, st = logits[:, tiles, :], rstat[:, tiles]
                dve.wait_ge(r_exp, b + 1)
                if b == 0:
                    dve.wait_ge(consts, 1)
                link(dve.tensor_reduce(st, lg, AX.X, ALU.add))
                link(dve.reciprocal(st, st))
                link(dve.tensor_tensor(lg, lg, st.unsqueeze(2).to_broadcast([P, QT, E]), ALU.mult))
                for t in range(b * QT, (b + 1) * QT):
                    last = dve.max(top[:, t, :], logits[:, t, :])
                link(last)
                for t in range(b * QT, (b + 1) * QT):
                    last = dve.max_index(top_i[:, t, :], top[:, t, :], logits[:, t, :])
                link(last)
                link(dve.tensor_copy(top_f[:, tiles, :], top_i[:, tiles, 0:TOPK]))
                link(dve.tensor_reduce(st, top[:, tiles, 0:TOPK], AX.X, ALU.add))
                link(dve.tensor_scalar(st, st, 1e-12, None, ALU.max))
                link(dve.reciprocal(st, st))
                dve.tensor_tensor(xrow[:, tiles, M_WEIGHT:M_WEIGHT + TOPK], top[:, tiles, 0:TOPK],
                                  st.unsqueeze(2).to_broadcast([P, QT, TOPK]), ALU.mult)
                oh = onehot[:, tiles, :, :].rearrange("p t j e -> p (t j) e")
                link(dve.tensor_tensor(oh, iota_e[:, :].unsqueeze(1).to_broadcast([P, QT * TOPK, E]),
                                       top_f[:, tiles, :].rearrange("p t j -> p (t j)").unsqueeze(2).to_broadcast([P, QT * TOPK, E]),
                                       ALU.is_equal))
                with nc.allow_low_precision(reason="zeros and ones are exact"):
                    dve.tensor_reduce(mask[:, tiles, :], onehot[:, tiles, :, :].rearrange("p t j e -> p t e j"), AX.X,
                                      ALU.add).then_inc(mask_rdy, 1)

            for s in slots():
                n = s + AHEAD
                if 0 <= n < ALL:
                    g, b, h, t, j = unit(n)
                    if n % UNITS == 0 and g >= 2:
                        dve.wait_ge(msp, g - 1)
                    dve.wait_ge(m_full, n + 1)
                    dve.tensor_reduce(mx[:, g % 2, t * GH + j:t * GH + j + 1], m_bank[n % M_BANKS][:, :], AX.X, ALU.max,
                                      negate=True).then_inc(m_done, 1)
                for st in STAGES_AT.get(s - 1, ()):
                    stage(*st)
                for (which, b), slot in NORM_SLOTS.items():
                    if s == slot:
                        norm_statistics(which, b)
                    if s == slot + NORM_GAP:
                        norm_scaling(which, b)
                for b, slot in ROUTE_SLOT.items():
                    if s == slot + 1:
                        route_sub(b)
                    if s == slot + 3:
                        route(b)

            dve.wait_ge(ranks, 1)
            link(dve.tensor_scalar(cnt_i[:, :], s_bank[2][0:E, 0:1], float(P - 1), None, ALU.add))
            link(dve.tensor_scalar(cnt_i[:, :], cnt_i[:, :], P.bit_length() - 1, None, ALU.logical_shift_right))
            dve.tensor_copy(tiles_b[:, :], cnt_i[:, 0:1].to_broadcast([E, P])).then_inc(tiles_rdy, 1)
            dve.wait_ge(bases, 1)
            link(dve.tensor_scalar(tile_cmp[:, :], s_bank[2][:, 64 + E:64 + 2 * E], iota_p[:, 0:1], None, ALU.is_le))
            link(dve.tensor_reduce(tile_e[:, :], tile_cmp[:, :], AX.X, ALU.add))
            link(dve.tensor_scalar(base[:, :], s_bank[2][:, 64:64 + E], float(P), None, ALU.mult))
            dve.tensor_scalar(tile_eb[:, :], tile_e[:, :], float(E - 1), None, ALU.min).then_inc(tile_e_rdy, 1)
            link(dve.tensor_tensor(pos, misc[:, :].rearrange("p (t e) -> p t e", t=NT),
                                   base[:, :].unsqueeze(1).to_broadcast([P, NT, E]), ALU.add))
            p4 = prod.rearrange("p (t j e) -> p t j e", t=NT, j=TOPK)
            link(dve.tensor_tensor(p4, onehot[:, :, :, :], pos.unsqueeze(2).to_broadcast([P, NT, TOPK, E]), ALU.mult))
            link(dve.tensor_reduce(slot_f[:, :], prod.rearrange("p (n e) -> p n e", e=E), AX.X, ALU.add))
            link(dve.tensor_copy(slot_i[:, :], slot_f[:, :]))
            dve.tensor_scalar(xrow[:, :, M_SLOT:M_SLOT + TOPK], slot_f[:, :].rearrange("p (t j) -> p t j", j=TOPK),
                              1.0, None, ALU.add).then_inc(slots_rdy, 1)
            dve.wait_ge(tile_row, 1)
            dve.tensor_scalar(offs[:, :], s_bank[2][0:1, 256:256 + SLOT_TILES], float(WORDS), None, ALU.mult)\
                .then_inc(offs_rdy, 1)

            def shared_sum(b):
                dve.wait_ge(sd_full, SC * (b + 1))
                for i in range(2):
                    r = xres[:, b * QT + 2 * i:b * QT + 2 * i + 2, :]
                    dve.tensor_tensor(r, o_bank[i][:, :].rearrange("p (t n) -> p t n", t=2), r, ALU.add).then_inc(sd_out, 1)

            for k in range(B * SC):
                if k >= SC and k % SC == 1:
                    shared_sum(k // SC - 1)
                dve.wait_ge(sg_act, k + 1)
                if k >= SC:
                    dve.wait_ge(sd_full, k - SC + 1)
                dve.tensor_tensor(hid[:, k % SC, :], m_bank[k % 2][:, :], gated[k % 2], ALU.mult).then_inc(sg_hid, 1)
            shared_sum(B - 1)

            def destinations():
                dve.wait_ge(ld_meta, 16)
                shape = [P, SLOT_TILES, TOPK]
                link(dve.tensor_tensor(mine[:, :, :], meta[:, :, 0:TOPK], my_slot[:, :].unsqueeze(2).to_broadcast(shape),
                                       ALU.is_equal))
                dve.tensor_tensor(mtmp[:, :, :], mine[:, :, :], meta[:, :, TOPK:2 * TOPK], ALU.mult)
                link(dve.tensor_reduce(found[:, :], mine[:, :, :], AX.X, ALU.add))
                link(dve.tensor_reduce(wgt[:, :], mtmp[:, :, :], AX.X, ALU.add))
                link(dve.tensor_tensor(mtmp[:, :, :], mine[:, :, :], iota_j[:, :].unsqueeze(1).to_broadcast(shape), ALU.mult))
                link(dve.tensor_reduce(dest_f[:, :], mtmp[:, :, :], AX.X, ALU.add))
                link(dve.scalar_tensor_tensor(out=dest_f[:, :], in0=meta[:, :, 2 * TOPK], scalar=float(TOPK), in1=dest_f[:, :],
                                              op0=ALU.mult, op1=ALU.add))
                link(dve.tensor_tensor(dest_f[:, :], dest_f[:, :], dummy[:, :], ALU.subtract))
                link(dve.tensor_tensor(dest_f[:, :], dest_f[:, :], found[:, :], ALU.mult))
                dve.tensor_tensor(dest[:, :], dest_f[:, :], dummy[:, :], ALU.add).then_inc(dest_rdy, 1)

            def step(k, r):
                fixed = isinstance(k, int)
                if not fixed or k < SLOT_TILES:
                    dve.wait_ge(x_full, k + 1)
                    dve.tensor_copy(xT[r % 2], s_bank[r % 2][:, 0:D].rearrange("p (c t) -> p c t", c=C)).then_inc(x_rdy, 1)
                if not fixed or 1 <= k <= SLOT_TILES:
                    q = (r - 1) % 2
                    dve.wait_ge(g_act, k)
                    dve.tensor_tensor(hidden[q], m_bank[q][:, EH:2 * EH], gate[q], ALU.mult).then_inc(h_rdy, 1)

            for k in range(UNROLL):
                step(k, k)
                if k == 2:
                    destinations()
            with dve.Fori(1, SLOT_TILES // UNROLL) as i:
                for r in range(UNROLL):
                    step(i * UNROLL + r, r)
            step(SLOT_TILES, 0)

            for t in range(NT):
                z, a = zring[t % 4], zsum[t % 2]
                dve.wait_ge(ld_z[t % 4], 16 * (t // 4 + 1))
                link(dve.tensor_tensor(a, z[:, 0:2, :], z[:, 2:4, :], ALU.add))
                link(dve.tensor_tensor(a[:, 0, :], a[:, 0, :], a[:, 1, :], ALU.add))
                dve.tensor_tensor(xres[:, t, :], xres[:, t, :], a[:, 0, :], ALU.add).then_inc(z_sum, 1)


def kernel(x, ctx_1024, L0_xattn_Wk, L0_xattn_bk, L0_xattn_Wq, L0_xattn_bq, L0_xattn_Wc, L0_xattn_bc, L0_ffn_router_w,
           L0_ffn_router_bias, L0_ffn_gate_w, L0_ffn_up_w, L0_ffn_down_w, L0_ffn_sgate_w, L0_ffn_sup_w, L0_ffn_sdown_w):
    import numpy as np
    import concourse.bacc as bacc
    from concourse.bass_utils import run_bass_kernel_spmd

    def flat(a):
        return np.ascontiguousarray(np.asarray(a).reshape(N, D))

    def turned(a):
        return np.ascontiguousarray(np.asarray(a).T)

    def columns(a):
        return np.ascontiguousarray(np.asarray(a).reshape(C, P).T)

    def spread(a):
        return np.ascontiguousarray(np.broadcast_to(np.asarray(a), (P, a.shape[0])))

    gate, up, down = (np.asarray(a).transpose(2, 0, 1) for a in (L0_ffn_gate_w, L0_ffn_up_w, L0_ffn_down_w))
    wall = np.concatenate([m[c * P:(c + 1) * P] for c in range(C) for m in (gate, up)] + [down], axis=2)
    arrays = dict(
        x=flat(x), ctxn=flat(ctx_1024), ctxT=turned(flat(ctx_1024)),
        wkT=turned(L0_xattn_Wk), wqT=turned(L0_xattn_Wq), wcT=turned(L0_xattn_Wc),
        bk=columns(L0_xattn_bk), bq=columns(L0_xattn_bq), bc=spread(L0_xattn_bc),
        rwT=turned(L0_ffn_router_w), rb=spread(L0_ffn_router_bias),
        sgT=turned(L0_ffn_sgate_w), suT=turned(L0_ffn_sup_w), sdT=turned(L0_ffn_sdown_w),
        wall=np.ascontiguousarray(wall.reshape(P, E * WORDS)),
    )
    nc = bacc.Bacc("TRN2", target_bir_lowering=False, num_devices=1)
    aps = {n: nc.dram_tensor(f"in_{n}", a.shape, F32, kind="ExternalInput").ap() for n, a in arrays.items()}
    out = nc.dram_tensor("out_rows", (N, D), F32, kind="ExternalOutput").ap()
    build(nc, out=out, **aps)
    r = run_bass_kernel_spmd(nc, [{f"in_{n}": a for n, a in arrays.items()}], core_ids=[0])
    return r.results[0]["out_rows"].reshape(B, T, D)
```

```python
from contextlib import ExitStack

import concourse.bass as bass
from concourse import mybir

ALU = mybir.AluOpType
ACT = mybir.ActivationFunctionType
AX = mybir.AxisListType
F32 = mybir.dt.float32
BF16 = mybir.dt.bfloat16
I32 = mybir.dt.int32
U32 = mybir.dt.uint32

P = 128
B, T, D = 4, 512, 256
N = B * T
H, HD = 16, 16
C = D // P
QT = T // P
NT = N // P
E, EH, TOPK = 32, 128, 4
SH = 512
SC = SH // P
SCALE = HD ** -0.5
LN_EPS = 1e-5

Q_PART = (0, 0, 1, 0, 2, 1)
K_PART = (0, 1, 0, 2, 0, 1)
BLOCKS = len(Q_PART)
SHIFT_ROW = BLOCKS * HD
ROWS = SHIFT_ROW + 3

GH = 4
GROUPS = B * H // GH
BG = H // GH
UNITS = QT * GH
ALL = GROUPS * UNITS
AHEAD = 28
LAG = 4
S_BANKS, M_BANKS = 3, 2
P_RING = 8

UNROLL = 4
SLOT_TILES = -(-((N * TOPK + E * (P - 1)) // P) // UNROLL) * UNROLL
SLOTS = SLOT_TILES * P
WORDS = 3 * D
M_SLOT, M_WEIGHT, M_TOKEN, ROW = D, D + TOPK, D + 2 * TOPK, D + 2 * TOPK + 1
META = ROW - D
FILLS = 8
FILL_TILES = SLOT_TILES // FILLS
DEPTH = 3


def stage_plan():
    at = {}

    def put(slot, name, *arg):
        at.setdefault(slot, []).append((name, *arg))

    for u, stage in enumerate((("K", 0, 0), ("K", 0, 1), ("NT", 0, 0), ("NT", 0, 1), ("Q", 0, 0), ("Q", 0, 1),
                               ("NT", 1, 0), ("NT", 1, 1), ("K", 1, 0), ("K", 1, 1))):
        put(-AHEAD - 12 + u, *stage)
    for b in range(1, B):
        s = UNITS * BG * (b - 1)
        if b >= 2:
            put(s - 32, "NT", b, 0)
            put(s - 29, "NT", b, 1)
            put(s - 16, "K", b, 0)
            put(s - 5, "K", b, 1)
        put(s - (2 if b >= 2 else 16), "Q", b, 0)
        put(s + 3 if b >= 2 else s - 10, "Q", b, 1)
    for g in range(GROUPS):
        put(UNITS * g - 7, "MR", g)
        put(UNITS * (g + 1) + 6, "YT", g)
    for b in range(B):
        s = UNITS * BG * (b + 1)
        for u, name, c in ((11, "AT", 0), (14, "AT", 1), (19, "WC", 0), (27, "WC", 1),
                           (43, "XT", 0), (46, "XT", 1), (51, "LG", 0)):
            put(s + u, name, b, c)
    return at


STAGES_AT = stage_plan()
FIRST_SLOT = min(STAGES_AT)
LAST_SLOT = max(STAGES_AT) + 14
ROUTE_SLOT = {b: UNITS * BG * (b + 1) + 51 for b in range(B)}
STAGE_NO = {}
for _s in range(FIRST_SLOT, LAST_SLOT + 1):
    for _st in STAGES_AT.get(_s, ()):
        STAGE_NO[_st] = len(STAGE_NO)


def through(*stage):
    return STAGE_NO[stage] + 1


NORM_SLOTS = {(1, 0): FIRST_SLOT, (1, 1): FIRST_SLOT + 3}
for _b in range(2, B):
    NORM_SLOTS[(1, _b)] = UNITS * BG * (_b - 1) - 45
for _b in range(B):
    NORM_SLOTS[(2, _b)] = UNITS * BG * (_b + 1) + 29
NORM_NO = {k: n for n, k in enumerate(sorted(NORM_SLOTS, key=NORM_SLOTS.get))}


FILL_SLOTS = [UNITS * (BG * _b + _g) + 10 for _b in range(B) for _g in (1, 2)]


def norm_gap(which, b):
    return int(which == 2 or b >= 2)


def unit(n):
    g, u = divmod(n, UNITS)
    t, j = divmod(u, GH)
    return g, g // BG, g % BG * GH + j, t, j


def build(nc, x, ctxn, ctxT, wkT, wqT, wcT, bk, bq, bc, rwT, rb, sgT, suT, sdT, wall, out):
    slot_rows = nc.dram_tensor("slot_rows", (SLOTS, ROW), F32, kind="Internal").ap()
    choice_rows = nc.dram_tensor("choice_rows", (N * TOPK + SLOTS, D), F32, kind="Internal").ap()
    parts_d = nc.dram_tensor("parts", (B, 2, 3, D, T), BF16, kind="Internal").ap()
    with ExitStack() as ctx:
        def sb(name, shape, dt=F32):
            return ctx.enter_context(nc.sbuf_tensor(name, shape, dt))

        def ps(name, shape, dt=F32):
            return ctx.enter_context(nc.psum_tensor(name, shape, dt))

        def sem(name):
            return ctx.enter_context(nc.semaphore(name))

        weights = sb("weights", [P, E * WORDS])
        words = H * T // 2
        qs = [weights[:, i * words:(i + 1) * words].bitcast(BF16).rearrange("p (h t) -> p h t", h=H) for i in (0, 1)]
        ks = [weights[:, i * words:(i + 1) * words].bitcast(BF16).rearrange("p (h t) -> p h t", h=H) for i in (2, 3)]
        at = 4 * words
        vwords = QT * H * 32
        vaug = [weights[:, at + i * vwords:at + (i + 1) * vwords].rearrange("p (k h m) -> p k h m", k=QT, h=H)
                for i in (0, 1)]
        at += 2 * vwords
        expo = [weights[:, at + i * T:at + (i + 1) * T] for i in range(P_RING)]
        assert at + P_RING * T <= E * WORDS

        xres = sb("xres", [P, NT, D])
        xrow = sb("xrow", [P, NT, ROW])
        xn2T = sb("xn2T", [P, C, N])
        early = sb("early", [P, 6 * C * T])
        late = sb("late", [P, 4 * C * T])

        def cut(arena, sizes):
            at, got = 0, []
            for n in sizes:
                got.append(arena[:, at:at + n])
                at += n
            assert at <= arena.shape[1]
            return got

        def chunks(ap, n):
            return ap.rearrange("p (c n) -> p c n", c=n)

        cT, cn, xnT, full0, full1, rest, part0, part1 = cut(early, [C * T] * 3 + [T] * 3 + [3 * T // 2] * 2)
        cT, cn, xnT = chunks(cT, C), chunks(cn, QT), chunks(xnT, C)
        full = [full0, full1]
        part = [chunks(p.bitcast(BF16), 3) for p in (part0, part1)]
        o_sb, y, yT, wk, wq, wc = cut(late, [T, C * T, C * T, C * D, C * D, C * D])
        y, yT, wk, wq, wc = chunks(y, QT), chunks(yT, C), chunks(wk, C), chunks(wq, C), chunks(wc, C)

        sg, su, sd, gated0, gated1, hid = cut(early, [C * SH] * 2 + [SC * D] + [T] * 2 + [SC * T])
        sg, su, sd, hid = chunks(sg, C), chunks(su, C), chunks(sd, SC), chunks(hid, SC)
        gated = [gated0, gated1]
        prod, pos, xg = cut(late, [NT * TOPK * E, NT * E, UNROLL * D])
        pos, xg = chunks(pos, NT), chunks(xg, UNROLL)
        ring = cut(late, [UNROLL * D, C * P, C * P, P, P, P, P])
        yo, xT, gate, hidden = chunks(ring[0], UNROLL), [chunks(r, C) for r in ring[1:3]], ring[3:5], ring[5:7]
        hiddenT = [sb(f"hiddenT{i}", [P, EH]) for i in range(2)]
        meta, mine, mtmp = (chunks(m, SLOT_TILES)
                            for m in cut(early, [SLOT_TILES * META, SLOT_TILES * TOPK, SLOT_TILES * TOPK]))
        zring = [chunks(z, TOPK) for z in cut(early, [TOPK * D] * 4)]
        zsum = [chunks(z, 2) for z in cut(early, [TOPK * D] * 4 + [2 * D] * 2)[4:]]

        bk_s = sb("bk_s", [P, C])
        bq_s = sb("bq_s", [P, C])
        bc_s = sb("bc_s", [P, D])
        rw_s = sb("rw_s", [P, C, E])
        rb_s = sb("rb_s", [P, E])
        ident = sb("ident", [P, P])
        identb = sb("identb", [P, P], BF16)
        stats = sb("stats", [P, QT, 6])
        mv = sb("mv", [P, QT, 2])
        rstd = sb("rstd", [P, QT])
        minus_half = sb("minus_half", [P, QT])
        mx = sb("mx", [P, 2, UNITS])
        mres = sb("mres", [P, UNITS])
        msplit = sb("msplit", [P, QT, 3, GH], BF16)
        mrow = sb("mrow", [3 * GH, T], BF16)
        ones = sb("ones", [3, T], BF16)
        den = sb("den", [P, QT, GH])
        logits = sb("logits", [P, NT, E])
        top = sb("top", [P, NT, 8])
        top_i = sb("top_i", [P, NT, 8], U32)
        top_f = sb("top_f", [P, NT, TOPK])
        rstat = sb("rstat", [P, NT])
        onehot = sb("onehot", [P, NT, TOPK, E], BF16)
        mask = sb("mask", [P, NT, E], BF16)
        zeros = sb("zeros", [P, ROW])
        iota_i = sb("iota_i", [P, SLOT_TILES], I32)
        iota_e = sb("iota_e", [P, E])
        iota_p = sb("iota_p", [P, 1])
        iota_j = sb("iota_j", [P, TOPK])
        my_slot = sb("my_slot", [P, SLOT_TILES])
        dummy = sb("dummy_row", [P, SLOT_TILES])
        before = sb("before", [P, P], BF16)
        upto = sb("upto", [E, 2, E], BF16)
        onesb = sb("onesb", [P, P], BF16)
        cnt_i = sb("cnt_i", [E, 1], I32)
        tiles_b = sb("tiles_b", [E, P], BF16)
        base = sb("base", [P, E])
        tile_cmp = sb("tile_cmp", [P, E])
        tile_e = sb("tile_e", [P, 1])
        tile_eb = sb("tile_eb", [P, 1], BF16)
        offs = sb("offs", [1, SLOT_TILES], I32)
        slot_f = sb("slot_f", [P, NT * TOPK])
        slot_i = sb("slot_i", [P, NT * TOPK], I32)
        wgt = sb("wgt", [P, SLOT_TILES])
        found = sb("found", [P, SLOT_TILES])
        dest_f = sb("dest_f", [P, SLOT_TILES])
        dest = sb("dest", [P, SLOT_TILES], I32)
        dest_k = [sb(f"dest_k{i}", [P, 1], I32) for i in range(UNROLL)]

        s_bank = [ps(f"s_bank{i}", [P, T]) for i in range(S_BANKS)]
        m_bank = [ps(f"m_bank{i}", [P, T]) for i in range(M_BANKS)]
        o_bank = [ps(f"o_bank{i}", [P, T]) for i in range(2)]
        misc = ps("misc", [P, T])
        miscb = misc[:, :].bitcast(BF16)

        ld_x = [sem(f"ld_x{b}") for b in range(B)]
        ld_cT = sem("ld_cT")
        ld_cn = sem("ld_cn")
        ld_wk = sem("ld_wk")
        ld_wq = sem("ld_wq")
        ld_b = sem("ld_b")
        ld_wc = sem("ld_wc")
        idents = sem("idents")
        ones_rdy = sem("ones_rdy")
        ones_in = sem("ones_in")
        norm1 = sem("norm1")
        misc_full = sem("misc_full")
        misc_free = sem("misc_free")
        full_rdy = sem("full_rdy")
        split = sem("split")
        parts_out = [sem(f"parts_out{i}") for i in range(2)]
        opnd = [sem(f"opnd{i}") for i in range(2)]
        v_rdy = sem("v_rdy")
        m_full = sem("m_full")
        m_done = sem("m_done")
        msp = sem("msp")
        shift = [sem(f"shift{i}") for i in range(2)]
        s_full = sem("s_full")
        exp_done = sem("exp_done")
        pv_done = sem("pv_done")
        o_rdy = sem("o_rdy")
        norm2 = sem("norm2")
        rstd_rdy = sem("rstd_rdy")
        scaled = sem("scaled")
        resid = sem("resid")
        var1 = sem("var1")
        dchain = sem("dchain")
        pchain = sem("pchain")
        stored = sem("stored")
        filled = sem("filled")
        ld_sh = sem("ld_sh")
        ld_w = sem("ld_w")
        zero_rdy = sem("zero_rdy")
        consts = sem("consts")
        r_sub = sem("r_sub")
        r_exp = sem("r_exp")
        mask_rdy = sem("mask_rdy")
        ranks = sem("ranks")
        tiles_rdy = sem("tiles_rdy")
        bases = sem("bases")
        tile_e_rdy = sem("tile_e_rdy")
        tile_row = sem("tile_row")
        offs_rdy = sem("offs_rdy")
        slots_rdy = sem("slots_rdy")
        scattered = sem("scattered")
        ld_meta = sem("ld_meta")
        dest_rdy = sem("dest_rdy")
        sg_full = sem("sg_full")
        sg_act = sem("sg_act")
        sg_hid = sem("sg_hid")
        sd_full = sem("sd_full")
        sd_out = sem("sd_out")
        ld_xg = [sem(f"ld_xg{i}") for i in range(UNROLL)]
        x_full = sem("x_full")
        x_rdy = sem("x_rdy")
        g_full = sem("g_full")
        g_act = sem("g_act")
        h_rdy = sem("h_rdy")
        ht_full = sem("ht_full")
        ht_rdy = sem("ht_rdy")
        y_full = sem("y_full")
        yo_rdy = sem("yo_rdy")
        dest_cp = sem("dest_cp")
        z_out = [sem(f"z_out{i}") for i in range(UNROLL)]
        ld_z = [sem(f"ld_z{i}") for i in range(4)]
        z_sum = sem("z_sum")

        block = ctx.enter_context(nc.Block())

        def slots():
            return range(FIRST_SLOT, LAST_SLOT + 1)

        def projection_no(b, name, c):
            return 4 * b + 2 * (name == "Q") + c

        def split_projection(eng, link, b, name, c):
            n = projection_no(b, name, c)
            eng.wait_ge(misc_free, through(name, b, c))
            eng.wait_ge(full_rdy, n + 1)
            if n:
                eng.wait_ge(split, n)
            f, p = full[n % 2], part[n % 2]
            link(eng.tensor_tensor(rest[:, :], f[:, :], p[:, 0, :], ALU.subtract))
            link(eng.tensor_copy(p[:, 1, :], rest[:, :]))
            eng.tensor_tensor(p[:, 2, :], rest[:, :], p[:, 1, :], ALU.subtract).then_inc(split, 1)

        @block.sync
        def _(sp):
            def load_ctx(b):
                if b:
                    sp.wait_ge(misc_full, through("K", b - 1, 1))
                sp.dma_start(cT[:, :, :], ctxT[:, b * T:(b + 1) * T].rearrange("(c p) t -> p c t", p=P)).then_inc(ld_cT, 16)

            def load_values(b):
                if b:
                    sp.wait_ge(v_rdy, b)
                sp.dma_start(cn[:, :, :], ctxn[b * T:(b + 1) * T, :].rearrange("(k p) d -> p k d", p=P)).then_inc(ld_cn, 16)

            def load_x(b):
                sp.dma_start(xres[:, b * QT:(b + 1) * QT, :],
                             x[b * T:(b + 1) * T, :].rearrange("(k p) d -> p k d", p=P)).then_inc(ld_x[b], 16)

            sp.dma_start(wk[:, :, :], wkT.rearrange("(c p) n -> p c n", p=P)).then_inc(ld_wk, 16)
            load_ctx(0)
            load_values(0)
            load_x(0)
            sp.dma_start(bk_s[:, :], bk).then_inc(ld_b, 16)
            sp.dma_start(bq_s[:, :], bq).then_inc(ld_b, 16)
            sp.dma_start(wq[:, :, :], wqT.rearrange("(c p) n -> p c n", p=P)).then_inc(ld_wq, 16)
            sp.wait_ge(ones_rdy, 1)
            for i in range(2):
                sp.dma_start(ks[i][SHIFT_ROW:ROWS, :, :], ones[:, :].unsqueeze(1).to_broadcast([3, H, T])).then_inc(ones_in, 16)
            load_x(1)
            load_x(2)
            load_x(3)
            sp.dma_start(wc[:, :, :], wcT.rearrange("(c p) n -> p c n", p=P)).then_inc(ld_wc, 16)
            sp.dma_start(bc_s[:, :], bc).then_inc(ld_wc, 16)
            sp.dma_start(rw_s[:, :, :], rwT.rearrange("(c p) n -> p c n", p=P)).then_inc(ld_wc, 16)
            sp.dma_start(rb_s[:, :], rb).then_inc(ld_wc, 16)

            def store_parts(b, name, c):
                n = projection_no(b, name, c)
                sp.wait_ge(split, n + 1)
                sp.dma_start(parts_d[b, int(name == "Q"), :, c * P:(c + 1) * P, :].rearrange("s p t -> p s t"),
                             part[n % 2][:, :, :]).then_inc(parts_out[n % 2], 16)

            def stack(b, name):
                n = projection_no(b, name, 1)
                sp.wait_ge(parts_out[0], 8 * (n + 1))
                sp.wait_ge(parts_out[1], 8 * (n + 1))
                if b >= 2:
                    sp.wait_ge(s_full, UNITS * BG * (b - 1))
                dst, which = (qs[b % 2], Q_PART) if name == "Q" else (ks[b % 2], K_PART)
                for i, s in enumerate(which):
                    sp.dma_start(dst[i * HD:(i + 1) * HD, :, :],
                                 parts_d[b, int(name == "Q"), s].rearrange("(h d) t -> d h t", d=HD)).then_inc(opnd[b % 2], 16)

            def shift_rows(g):
                b, gg = divmod(g, BG)
                sp.wait_ge(misc_free, through("MR", g))
                for s in range(3):
                    sp.dma_start(qs[b % 2][SHIFT_ROW + s:SHIFT_ROW + s + 1, gg * GH:(gg + 1) * GH, :],
                                 mrow[s * GH:(s + 1) * GH, :]).then_inc(shift[g % 2], 16)

            for s in slots():
                for name, *arg in STAGES_AT.get(s, ()):
                    if name in ("K", "Q"):
                        b, c = arg
                        store_parts(b, name, c)
                        if (name, c) == ("K", 1) and b + 1 < B:
                            load_ctx(b + 1)
                        if c == 1 and b == 0:
                            stack(b, name)
                            if name == "K":
                                load_values(1)
                    if name == "MR":
                        shift_rows(*arg)
                if s == 8:
                    load_values(2)
                if s == UNITS * BG + 12:
                    load_values(3)
                if s in FILL_SLOTS:
                    i = FILL_SLOTS.index(s)
                    if i == 0:
                        sp.wait_ge(zero_rdy, 1)
                    sp.dma_start(slot_rows[i * FILL_TILES * P:(i + 1) * FILL_TILES * P, :].rearrange("(t p) r -> p t r", p=P),
                                 zeros[:, :].unsqueeze(1).to_broadcast([P, FILL_TILES, ROW])).then_inc(filled, 16)
                if s == UNITS * BG * (B - 2) + 20:
                    sp.wait_ge(misc_full, through("Q", B - 1, 1))
                    sp.wait_ge(v_rdy, B)
                    sp.wait_ge(split, 4 * B)
                    for i in range(2):
                        sp.wait_ge(parts_out[i], 16 * 2 * B)
                    sp.dma_start(sg, sgT.rearrange("(c p) n -> p c n", p=P)).then_inc(ld_sh, 16)
                    sp.dma_start(su, suT.rearrange("(c p) n -> p c n", p=P)).then_inc(ld_sh, 16)
                    sp.dma_start(sd, sdT.rearrange("(c p) n -> p c n", p=P)).then_inc(ld_sh, 16)
                if s == ALL:
                    sp.wait_ge(pv_done, ALL)
                    q = E * WORDS // 4
                    for i in range(4):
                        sp.dma_start(weights[:, i * q:(i + 1) * q], wall[:, i * q:(i + 1) * q]).then_inc(ld_w, 16)
                b, u = divmod(s, UNITS * BG)
                if 1 <= b + 1 < B and (b or u):
                    if u == 10:
                        stack(b + 1, "K")
                    if u == 15:
                        stack(b + 1, "Q")

            sp.wait_ge(scattered, 16 * NT * TOPK)

            def load_rows(k, r):
                if not isinstance(k, int) or k >= UNROLL:
                    sp.wait_ge(x_full, k - UNROLL + 1)
                sp.dma_start(xg[:, r, :], slot_rows[bass.ds(k * P, P), 0:D]).then_inc(ld_xg[r], 16)

            for k in range(UNROLL):
                load_rows(k, k)
            sp.wait_ge(sd_out, 2 * B)
            sp.dma_start(meta[:, :, :], slot_rows[:, D:ROW].rearrange("(t p) m -> p t m", p=P)).then_inc(ld_meta, 16)
            with sp.Fori(1, SLOT_TILES // UNROLL) as i:
                for r in range(UNROLL):
                    load_rows(i * UNROLL + r, r)

            for i in range(UNROLL):
                sp.wait_ge(z_out[i], 16 * (SLOT_TILES // UNROLL))
            for t in range(NT):
                if t >= 4:
                    sp.wait_ge(z_sum, t - 3)
                sp.dma_start(zring[t % 4], choice_rows[t * P * TOPK:(t + 1) * P * TOPK, :].rearrange("(p j) d -> p j d", j=TOPK))\
                    .then_inc(ld_z[t % 4], 16)

        @block.tensor
        def _(pe):
            def stage(name, *arg):
                no = STAGE_NO[(name, *arg)]
                if no:
                    pe.wait_ge(misc_free, no)
                if name in ("K", "Q"):
                    b, c = arg
                    if name == "K":
                        pe.wait_ge(ld_cT, 16 * (b + 1))
                        pe.wait_ge(ld_wk, 16)
                    else:
                        pe.wait_ge(misc_free, through("NT", b, 1))
                        pe.wait_ge(ld_wq, 16)
                    w, act = (wk, cT) if name == "K" else (wq, xnT)
                    for i in range(C):
                        mm = pe.matmul(misc[:, :], w[:, i, c * P:(c + 1) * P], act[:, i, :], start=i == 0, stop=i == C - 1)
                elif name == "NT":
                    b, c = arg
                    pe.wait_ge(norm1, b + 1)
                    pe.wait_ge(idents, 1)
                    for t in range(QT):
                        mm = pe.transpose(misc[:, t * P:(t + 1) * P], xrow[:, b * QT + t, c * P:(c + 1) * P], ident[:, :])
                elif name == "MR":
                    pe.wait_ge(msp, arg[0] + 1)
                    pe.wait_ge(idents, 2)
                    for t in range(QT):
                        mm = pe.transpose(miscb[0:3 * GH, t * P:(t + 1) * P], msplit[:, t, :, :].rearrange("p s j -> p (s j)"), identb[:, :])
                elif name == "YT":
                    pe.wait_ge(o_rdy, arg[0] + 1)
                    for t in range(QT):
                        mm = pe.transpose(misc[:, t * P:(t + 1) * P], o_sb[:, t * P:(t + 1) * P], ident[:, :])
                elif name == "AT":
                    b, c = arg
                    pe.wait_ge(misc_free, through("YT", BG * b + BG - 1))
                    for t in range(QT):
                        mm = pe.transpose(misc[:, t * P:(t + 1) * P], y[:, t, c * P:(c + 1) * P], ident[:, :])
                elif name == "WC":
                    b, half = arg
                    pe.wait_ge(misc_free, through("AT", b, 1))
                    pe.wait_ge(ld_wc, 64)
                    for t in range(2):
                        for i in range(C):
                            k = (2 * half + t) * P
                            mm = pe.matmul(misc[:, t * D:(t + 1) * D], yT[:, i, k:k + P], wc[:, i, :],
                                           start=i == 0, stop=i == C - 1)
                elif name == "XT":
                    b, c = arg
                    pe.wait_ge(norm2, b + 1)
                    for t in range(QT):
                        mm = pe.transpose(misc[:, t * P:(t + 1) * P], xrow[:, b * QT + t, c * P:(c + 1) * P], ident[:, :])
                elif name == "LG":
                    b = arg[0]
                    pe.wait_ge(misc_free, through("XT", b, 1))
                    for t in range(QT):
                        for i in range(C):
                            k = (b * QT + t) * P
                            mm = pe.matmul(misc[:, t * E:(t + 1) * E], xn2T[:, i, k:k + P], rw_s[:, i, :],
                                           start=i == 0, stop=i == C - 1)
                mm.then_inc(misc_full, 1)

            for s in slots():
                if 0 <= s < ALL:
                    g, b, h, t, j = unit(s)
                    if s == 0:
                        pe.wait_ge(ones_in, 32)
                    if s % UNITS == 0:
                        pe.wait_ge(shift[g % 2], 48 * (g // 2 + 1))
                    if s >= S_BANKS:
                        pe.wait_ge(exp_done, s - S_BANKS + 1)
                    pe.matmul(s_bank[s % S_BANKS][:, :], ks[b % 2][0:ROWS, h, t * P:(t + 1) * P], qs[b % 2][0:ROWS, h, :],
                              start=True, stop=True).then_inc(s_full, 1)
                n = s + AHEAD
                if 0 <= n < ALL:
                    g, b, h, t, j = unit(n)
                    if n % (UNITS * BG) == 0:
                        pe.wait_ge(opnd[b % 2], 16 * 2 * BLOCKS * (b // 2 + 1))
                    if n >= M_BANKS:
                        pe.wait_ge(m_done, n - M_BANKS + 1)
                    pe.matmul(m_bank[n % M_BANKS][:, :], qs[b % 2][0:SHIFT_ROW, h, t * P:(t + 1) * P],
                              ks[b % 2][0:SHIFT_ROW, h, :], start=True, stop=True).then_inc(m_full, 1)
                n = s - LAG
                if 0 <= n < ALL:
                    g, b, h, t, j = unit(n)
                    if n % (UNITS * BG) == 0:
                        pe.wait_ge(v_rdy, b + 1)
                    if n % UNITS == 0 and g >= 2:
                        pe.wait_ge(o_rdy, g - 1)
                    pe.wait_ge(exp_done, n + 1)
                    pe.matmul(o_bank[g % 2][32 * j:32 * (j + 1), :], vaug[b % 2][:, t, h, :], expo[n % P_RING],
                              start=t == 0, stop=t == QT - 1).then_inc(pv_done, 1)
                for st in STAGES_AT.get(s, ()):
                    stage(*st)

            pe.wait_ge(misc_free, through("LG", B - 1, 0))
            pe.wait_ge(mask_rdy, B)
            pe.wait_ge(consts, 1)
            m2 = mask[:, :, :].rearrange("p t e -> p (t e)")
            pe.matmul(misc[:, :], before[:, :], m2, start=True, stop=False)
            for t in range(1, NT):
                pe.matmul(misc[:, t * E:], onesb[:, :], m2[:, 0:(NT - t) * E], start=False, stop=t == NT - 1)
            pe.wait_ge(exp_done, ALL)
            small = s_bank[2]
            for t in range(NT):
                mm = pe.matmul(small[0:E, 0:1], mask[:, t, :], onesb[:, 0:1], start=t == 0, stop=t == NT - 1)
            mm.then_inc(ranks, 1)

            def shared_up(k):
                b, c = divmod(k, SC)
                if k >= 2:
                    pe.wait_ge(sg_hid, k - 1)
                for w, bank in ((sg, s_bank[k % 2]), (su, m_bank[k % 2])):
                    for i in range(C):
                        mm = pe.matmul(bank[:, :], w[:, i, c * P:(c + 1) * P], xn2T[:, i, b * T:(b + 1) * T],
                                       start=i == 0, stop=i == C - 1)
                mm.then_inc(sg_full, 1)

            def shared_down(k):
                b, c = divmod(k, SC)
                pe.wait_ge(sg_hid, k + 1)
                if c == 0 and b:
                    pe.wait_ge(sd_out, 2 * b)
                for t in range(QT):
                    mm = pe.matmul(o_bank[t // 2][:, t % 2 * D:(t % 2 + 1) * D], hid[:, c, t * P:(t + 1) * P], sd[:, c, :],
                                   start=c == 0 and t % 2 == 0, stop=c == SC - 1, skip_group_check=True)
                mm.then_inc(sd_full, 1)

            pe.wait_ge(ld_sh, 48)
            pe.wait_ge(m_done, ALL)
            pe.wait_ge(o_rdy, GROUPS)
            for k in range(B * SC):
                shared_up(k)
                if k == 0:
                    pe.wait_ge(tiles_rdy, 1)
                    pe.matmul(small[:, 64:64 + 2 * E], tiles_b[:, :], upto[:, :, :].rearrange("p a b -> p (a b)"),
                              start=True, stop=True).then_inc(bases, 1)
                if k == 1:
                    pe.wait_ge(tile_e_rdy, 1)
                    pe.matmul(small[0:1, 256:256 + SLOT_TILES], tile_eb[0:SLOT_TILES, 0:1], identb[0:SLOT_TILES, 0:SLOT_TILES],
                              start=True, stop=True).then_inc(tile_row, 1)
                if k:
                    shared_down(k - 1)
            shared_down(B * SC - 1)

            pe.wait_ge(sd_out, 2 * B)
            pe.wait_ge(offs_rdy, 1)
            pe.wait_ge(slots_rdy, 1)
            pe.wait_ge(ld_w, 64)
            y_bank = [s_bank[2], misc]

            def load_offsets(k, n):
                return nc.values_load_multi_w_load_instructions(
                    offs[0:1, bass.ds(k, n)], engines=(mybir.EngineType.PE,), min_val=0, max_val=(E - 1) * WORDS,
                    skip_runtime_bounds_check_because="the tiles' experts were clamped to E - 1 before they were multiplied")[1]

            def step(k, r, w1, w3):
                fixed = isinstance(k, int)
                if not fixed or k < SLOT_TILES:
                    pe.wait_ge(ld_xg[r], 16 * (k // UNROLL + 1) if fixed else (k - r) * (16 // UNROLL) + 16)
                    for i in range(C):
                        mm = pe.transpose(s_bank[r % 2][:, i * P:(i + 1) * P], xg[:, r, i * P:(i + 1) * P], ident[:, :])
                    mm.then_inc(x_full, 1)
                if not fixed or 1 <= k <= SLOT_TILES:
                    q = (r - 1) % 2
                    pe.wait_ge(x_rdy, k)
                    for i in range(C):
                        mm = pe.matmul(m_bank[q][:, 0:2 * EH], xT[q][:, i, :], weights[:, bass.ds(w1 + i * D, 2 * EH)],
                                       start=i == 0, stop=i == C - 1)
                    mm.then_inc(g_full, 1)
                if not fixed or 2 <= k <= SLOT_TILES + 1:
                    q = (r - 2) % 2
                    pe.wait_ge(h_rdy, k - 1)
                    pe.transpose(o_bank[q][:, 0:P], hidden[q], ident[:, :]).then_inc(ht_full, 1)
                if not fixed or 3 <= k <= SLOT_TILES + 2:
                    q = (r - 3) % 2
                    pe.wait_ge(ht_rdy, k - 2)
                    if not fixed or k >= 5:
                        pe.wait_ge(yo_rdy, k - 4)
                    pe.matmul(y_bank[q][:, 0:D], hiddenT[q][:, :], weights[:, bass.ds(w3 + C * D, D)],
                              start=True, stop=True).then_inc(y_full, 1)

            w = load_offsets(0, UNROLL - 1)
            for k in range(UNROLL):
                step(k, k, w[k - 1] if k else None, w[k - 3] if k >= 3 else None)
            with pe.Fori(1, SLOT_TILES // UNROLL) as i:
                w = load_offsets(i * UNROLL - 3, UNROLL + 2)
                for r in range(UNROLL):
                    step(i * UNROLL + r, r, w[r + 2], w[r])
            w = load_offsets(SLOT_TILES - 3, 3)
            for k in range(DEPTH):
                step(SLOT_TILES + k, k, w[2], w[k])

        @block.scalar
        def _(act):
            def stage(name, *arg):
                if name in ("K", "Q"):
                    b, c = arg
                    n = projection_no(b, name, c)
                    act.wait_ge(misc_full, through(name, *arg))
                    if n == 0:
                        act.wait_ge(ld_b, 32)
                    if n >= 2:
                        act.wait_ge(split, n - 1)
                        act.wait_ge(parts_out[n % 2], 16 * (n // 2))
                    bias = (bk_s if name == "K" else bq_s)[:, c:c + 1]
                    act.activation(full[n % 2][:, :], misc[:, :], ACT.Identity, bias=bias).then_inc(full_rdy, 1)
                    act.activation(part[n % 2][:, 0, :], misc[:, :], ACT.Identity, bias=bias).then_inc(misc_free, 1)
                elif name == "NT":
                    b, c = arg
                    act.wait_ge(misc_full, through(name, *arg))
                    act.copy(xnT[:, c, :], misc[:, :]).then_inc(misc_free, 1)
                elif name == "AT":
                    b, c = arg
                    act.wait_ge(misc_full, through(name, *arg))
                    act.copy(yT[:, c, :], misc[:, :]).then_inc(misc_free, 1)
                elif name == "XT":
                    b, c = arg
                    act.wait_ge(misc_full, through(name, *arg))
                    act.copy(xn2T[:, c, b * T:(b + 1) * T], misc[:, :]).then_inc(misc_free, 1)

            for s in slots():
                if 0 <= s < ALL:
                    act.wait_ge(s_full, s + 1)
                    if s >= P_RING:
                        act.wait_ge(pv_done, s - P_RING + 1)
                    act.activation(expo[s % P_RING], s_bank[s % S_BANKS][:, :], ACT.Exp, scale=SCALE).then_inc(exp_done, 1)
                g, u = divmod(s - LAG, UNITS)
                g -= 1
                if u == 0 and 0 <= g < GROUPS:
                    act.wait_ge(pv_done, UNITS * (g + 1))
                    if g:
                        act.wait_ge(misc_full, through("YT", g - 1))
                    act.copy(o_sb[:, :], o_bank[g % 2][:, :]).then_inc(o_rdy, 1)
                for st in STAGES_AT.get(s - 1, ()):
                    stage(*st)
                for b, slot in ROUTE_SLOT.items():
                    if s == slot + 2:
                        act.wait_ge(r_sub, b + 1)
                        lg = logits[:, b * QT:(b + 1) * QT, :]
                        act.activation(lg, lg, ACT.Exp).then_inc(r_exp, 1)

            for k in range(B * SC):
                act.wait_ge(sg_full, k + 1)
                if k >= 2:
                    act.wait_ge(sg_hid, k - 1)
                act.activation(gated[k % 2], s_bank[k % 2][:, :], ACT.Silu).then_inc(sg_act, 1)

            def step(k, r):
                fixed = isinstance(k, int)
                if not fixed or 1 <= k <= SLOT_TILES:
                    q = (r - 1) % 2
                    act.wait_ge(g_full, k)
                    act.activation(gate[q], m_bank[q][:, 0:EH], ACT.Silu).then_inc(g_act, 1)
                if not fixed or 2 <= k <= SLOT_TILES + 1:
                    q = (r - 2) % 2
                    act.wait_ge(ht_full, k - 1)
                    act.copy(hiddenT[q][:, :], o_bank[q][:, 0:P]).then_inc(ht_rdy, 1)
                if not fixed or 3 <= k <= SLOT_TILES + 2:
                    q, o = (r - 3) % 2, (r - 3) % UNROLL
                    if fixed and k == 3:
                        act.wait_ge(dest_rdy, 1)
                    act.wait_ge(y_full, k - 2)
                    if not fixed:
                        act.wait_ge(z_out[o], (k - r) * (16 // UNROLL) - (16 if r < DEPTH else 0))
                    elif k - 3 >= UNROLL:
                        act.wait_ge(z_out[o], 16 * ((k - 3) // UNROLL))
                    act.activation(yo[:, o, :], [s_bank[2], misc][q][:, 0:D], ACT.Copy,
                                   scale=wgt[:, bass.ds(k - 3, 1)]).then_inc(yo_rdy, 1)

            for k in range(2 * UNROLL):
                step(k, k % UNROLL)
            with act.Fori(2, SLOT_TILES // UNROLL) as i:
                for r in range(UNROLL):
                    step(i * UNROLL + r, r)
            for k in range(SLOT_TILES, SLOT_TILES + DEPTH):
                step(k, k % UNROLL)

            for t in range(NT):
                act.wait_ge(z_sum, t + 1)
                act.dma_start(out[t * P:(t + 1) * P, :], xres[:, t, :]).then_inc(stored, 16)
            act.wait_ge(stored, 16 * NT)

        @block.gpsimd
        def _(pool):
            chain = [0]

            def link(ins):
                chain[0] += 1
                ins.then_inc(pchain, 1)
                pool.wait_ge(pchain, chain[0])

            link(pool.memset(ident[:, :], 0.0))
            link(pool.affine_select(out=ident[:, :], in_=ident[:, :], compare_op=ALU.not_equal, fill=1.0, base=0,
                                    pattern=[[-1, P]], channel_multiplier=1))
            pool.tensor_copy(identb[:, :], ident[:, :]).then_inc(idents, 2)
            link(pool.memset(minus_half[:, :], -0.5))
            link(pool.memset(zeros[:, :], 0.0))
            pool.nop().then_inc(zero_rdy, 1)
            for i in range(2):
                link(pool.memset(vaug[i], 0.0))
                link(pool.memset(vaug[i][:, :, :, HD:HD + 1], 1.0))

            def values(b):
                pool.wait_ge(ld_cn, 16 * (b + 1))
                if b >= 2:
                    pool.wait_ge(pv_done, UNITS * BG * (b - 1))
                pool.tensor_copy(vaug[b % 2].rearrange("p k h m -> p (k h) m")[:, :, 0:HD],
                                 cn[:, :, :].rearrange("p k (h d) -> p (k h) d", h=H)).then_inc(v_rdy, 1)

            def constants():
                def indices(out, pattern, base, step):
                    n = out.shape[1]
                    i = iota_i[0:out.shape[0], 0:n]
                    link(pool.iota(i, pattern, base=base, channel_multiplier=step))
                    link(pool.tensor_copy(out, i))

                indices(iota_e[:, :], [[1, E]], 0, 0)
                indices(iota_p[:, :], [[1, 1]], 0, 1)
                indices(iota_j[:, :], [[1, TOPK]], 0, 0)
                indices(my_slot[:, :], [[P, SLOT_TILES]], 1, 1)
                indices(dummy[:, :], [[P, SLOT_TILES]], N * TOPK, 1)
                indices(top_f[:, :, 0], [[P, NT]], 0, 1)
                link(pool.memset(onesb[:, :], 1.0))
                link(pool.affine_select(out=before[:, :], in_=onesb[:, :], compare_op=ALU.is_gt, fill=0.0, base=0,
                                        pattern=[[1, P]], channel_multiplier=-1))
                link(pool.affine_select(out=upto[:, 0, :], in_=onesb[0:E, 0:E], compare_op=ALU.is_gt, fill=0.0, base=0,
                                        pattern=[[1, E]], channel_multiplier=-1))
                link(pool.affine_select(out=upto[:, 1, :], in_=onesb[0:E, 0:E], compare_op=ALU.is_ge, fill=0.0, base=0,
                                        pattern=[[1, E]], channel_multiplier=-1))
                pool.tensor_copy(xrow[:, :, M_TOKEN], top_f[:, :, 0]).then_inc(consts, 1)

            def add_bias(b):
                r = xres[:, b * QT:(b + 1) * QT, :]
                pool.tensor_tensor(r, r, bc_s[:, :].rearrange("p (o n) -> p o n", o=1).to_broadcast([P, QT, D]), ALU.add)\
                    .then_inc(resid, 1)

            def norm_scaling(which, b):
                no = NORM_NO[(which, b)]
                pool.wait_ge(var1, no + 1)
                link(pool.tensor_scalar(rstd[:, :], mv[:, :, 1], LN_EPS, None, ALU.add))
                power = pool.tensor_tensor(rstd[:, :], rstd[:, :], minus_half[:, :], ALU.pow)
                if no == 0:
                    power.then_inc(rstd_rdy, 1)
                    pool.wait_ge(norm1, 1)
                    pool.wait_ge(ld_wc, 64)
                    add_bias(0)
                    return
                link(power)
                if which == 2:
                    pool.wait_ge(misc_full, through("NT", b, 1))
                for t in range(QT):
                    last = pool.tensor_scalar(xrow[:, b * QT + t, 0:D], xres[:, b * QT + t, :], mv[:, t, 0:1],
                                              rstd[:, t:t + 1], ALU.subtract, ALU.mult)
                last.then_inc(norm1 if which == 1 else norm2, 1)
                pool.wait_ge(norm1 if which == 1 else norm2, b + 1)
                pool.nop().then_inc(scaled, 1)
                if which == 1:
                    add_bias(b)

            for s in slots():
                if s == 2:
                    constants()
                for (which, b), slot in NORM_SLOTS.items():
                    if s == slot + (QT + 1) * norm_gap(which, b):
                        norm_scaling(which, b)
                for name, *arg in STAGES_AT.get(s, ()):
                    if name in ("K", "Q") and arg[0]:
                        split_projection(pool, link, arg[0], name, arg[1])
                    if (name, *arg) == ("K", 0, 1):
                        values(0)
                    if (name, *arg) == ("K", 1, 1):
                        values(1)
                b, u = divmod(s, UNITS * BG)
                if u == LAG + 4 and b >= 1 and b + 1 < B:
                    values(b + 1)

            pool.wait_ge(slots_rdy, 1)
            pool.wait_ge(filled, 16 * FILLS)
            for t in range(NT):
                for j in range(TOPK):
                    n = t * TOPK + j
                    pool.indirect_dma_start(slot_rows, bass.IndirectOffsetOnAxis(ap=slot_i[:, n:n + 1], axis=0),
                                            xrow[:, t, :], None).then_inc(scattered, 16)
            pool.wait_ge(dest_rdy, 1)

            def fetch_destinations(k, r):
                if not isinstance(k, int) or k >= UNROLL:
                    pool.wait_ge(z_out[r], k // UNROLL * 16 if isinstance(k, int) else (k - r) * (16 // UNROLL))
                pool.tensor_copy(dest_k[r][:, :], dest[:, bass.ds(k, 1)]).then_inc(dest_cp, 1)

            def scatter(k, r):
                pool.wait_ge(yo_rdy, k + 1)
                pool.wait_ge(dest_cp, k + 1)
                if not isinstance(k, int) or k + 1 < SLOT_TILES:
                    fetch_destinations(k + 1, (r + 1) % UNROLL)
                pool.indirect_dma_start(choice_rows, bass.IndirectOffsetOnAxis(ap=dest_k[r][:, 0:1], axis=0),
                                        yo[:, r, :], None).then_inc(z_out[r], 16)

            fetch_destinations(0, 0)
            for k in range(UNROLL):
                scatter(k, k)
            with pool.Fori(1, SLOT_TILES // UNROLL - 1) as i:
                for r in range(UNROLL):
                    scatter(i * UNROLL + r, r)
            for k in range(SLOT_TILES - UNROLL, SLOT_TILES):
                scatter(k, k % UNROLL)

        @block.vector
        def _(dve):
            chain = [0]

            def link(ins):
                chain[0] += 1
                ins.then_inc(dchain, 1)
                dve.wait_ge(dchain, chain[0])

            dve.memset(ones[:, :], 1.0).then_inc(ones_rdy, 1)

            def split_maxima(g, step):
                m = mx[:, g % 2, :].rearrange("p (t j) -> p t j", t=QT)
                r = mres[:, :].rearrange("p (t j) -> p t j", t=QT)
                if step == 0:
                    dve.wait_ge(m_done, UNITS * (g + 1))
                    if g:
                        dve.wait_ge(misc_full, through("MR", g - 1))
                        dve.wait_ge(msp, g)
                    link(dve.tensor_copy(msplit[:, :, 0, :], m))
                elif step == 1:
                    link(dve.tensor_tensor(r, m, msplit[:, :, 0, :], ALU.subtract))
                elif step == 2:
                    link(dve.tensor_copy(msplit[:, :, 1, :], r))
                else:
                    dve.tensor_tensor(msplit[:, :, 2, :], r, msplit[:, :, 1, :], ALU.subtract).then_inc(msp, 1)

            def norm_statistics(which, b, t):
                no = NORM_NO[(which, b)]
                if t == 0:
                    if which == 1:
                        dve.wait_ge(ld_x[b], 16)
                    else:
                        dve.wait_ge(misc_free, through("WC", b, 1))
                last = dve.bn_stats(stats[:, t, :], xres[:, b * QT + t, :])
                if t == QT - 1:
                    link(last)
                    if no >= 2:
                        dve.wait_ge(scaled, no - 1)
                    for i in range(QT):
                        last = dve.bn_aggr(mv[:, i, :], stats[:, i, :])
                    last.then_inc(var1, 1)
                    if no == 0:
                        dve.wait_ge(rstd_rdy, 1)
                        for i in range(QT):
                            last = dve.tensor_scalar(xrow[:, i, 0:D], xres[:, i, :], mv[:, i, 0:1], rstd[:, i:i + 1],
                                                     ALU.subtract, ALU.mult)
                        last.then_inc(norm1, 1)
                        dve.wait_ge(norm1, 1)

            def stage(name, *arg):
                if name == "MR":
                    g, = arg
                    dve.wait_ge(misc_full, through(name, *arg))
                    if g:
                        dve.wait_ge(shift[(g - 1) % 2], 48 * ((g - 1) // 2 + 1))
                    dve.tensor_copy(mrow[:, :], miscb[0:3 * GH, 0:T]).then_inc(misc_free, 1)
                elif name == "YT":
                    g, = arg
                    dve.wait_ge(misc_full, through(name, *arg))
                    o = misc[:, :].rearrange("p (t j m) -> p t j m", t=QT, j=GH)
                    link(dve.reciprocal(den[:, :, :], o[:, :, :, HD]))
                    gg = g % BG
                    dve.tensor_tensor(y[:, :, gg * GH * HD:(gg + 1) * GH * HD].rearrange("p t (j d) -> p t j d", j=GH),
                                      o[:, :, :, 0:HD], den[:, :, :].unsqueeze(3).to_broadcast([P, QT, GH, HD]), ALU.mult)\
                        .then_inc(misc_free, 1)
                elif name == "WC":
                    b, half = arg
                    dve.wait_ge(misc_full, through(name, *arg))
                    dve.wait_ge(resid, b + 1)
                    r = xres[:, b * QT + 2 * half:b * QT + 2 * half + 2, :]
                    dve.tensor_tensor(r, misc[:, :].rearrange("p (t n) -> p t n", t=2), r, ALU.add).then_inc(misc_free, 1)
                elif name == "LG":
                    b = arg[0]
                    dve.wait_ge(misc_full, through(name, *arg))
                    dve.tensor_tensor(logits[:, b * QT:(b + 1) * QT, :], misc[:, 0:QT * E].rearrange("p (t e) -> p t e", t=QT),
                                      rb_s[:, :].unsqueeze(1).to_broadcast([P, QT, E]), ALU.add).then_inc(misc_free, 1)

            def route_sub(b):
                dve.wait_ge(misc_free, through("LG", b, 0))
                lg, st = logits[:, b * QT:(b + 1) * QT, :], rstat[:, b * QT:(b + 1) * QT]
                link(dve.tensor_reduce(st, lg, AX.X, ALU.max))
                dve.tensor_tensor(lg, lg, st.unsqueeze(2).to_broadcast([P, QT, E]), ALU.subtract).then_inc(r_sub, 1)

            def route(b, step):
                tiles = slice(b * QT, (b + 1) * QT)
                lg, st = logits[:, tiles, :], rstat[:, tiles]
                oh = onehot[:, tiles, :, :].rearrange("p t j e -> p (t j) e")
                if step == 0:
                    dve.wait_ge(r_exp, b + 1)
                    if b == 0:
                        dve.wait_ge(consts, 1)
                    link(dve.tensor_reduce(st, lg, AX.X, ALU.add))
                    link(dve.reciprocal(st, st))
                elif step == 1:
                    link(dve.tensor_tensor(lg, lg, st.unsqueeze(2).to_broadcast([P, QT, E]), ALU.mult))
                elif step == 2:
                    for t in range(b * QT, (b + 1) * QT):
                        last = dve.max(top[:, t, :], logits[:, t, :])
                    link(last)
                elif step == 3:
                    for t in range(b * QT, (b + 1) * QT):
                        last = dve.max_index(top_i[:, t, :], top[:, t, :], logits[:, t, :])
                    link(last)
                elif step == 4:
                    dve.tensor_copy(top_f[:, tiles, :], top_i[:, tiles, 0:TOPK])
                    link(dve.tensor_reduce(st, top[:, tiles, 0:TOPK], AX.X, ALU.add))
                    link(dve.tensor_scalar(st, st, 1e-12, None, ALU.max))
                elif step == 5:
                    link(dve.reciprocal(st, st))
                    dve.tensor_tensor(xrow[:, tiles, M_WEIGHT:M_WEIGHT + TOPK], top[:, tiles, 0:TOPK],
                                      st.unsqueeze(2).to_broadcast([P, QT, TOPK]), ALU.mult)
                elif step == 6:
                    link(dve.tensor_tensor(oh, iota_e[:, :].unsqueeze(1).to_broadcast([P, QT * TOPK, E]),
                                           top_f[:, tiles, :].rearrange("p t j -> p (t j)").unsqueeze(2)
                                           .to_broadcast([P, QT * TOPK, E]), ALU.is_equal))
                elif step == 7:
                    with nc.allow_low_precision(reason="zeros and ones are exact"):
                        dve.tensor_reduce(mask[:, tiles, :], onehot[:, tiles, :, :].rearrange("p t j e -> p t e j"), AX.X,
                                          ALU.add).then_inc(mask_rdy, 1)

            for s in slots():
                n = s + AHEAD
                if 0 <= n < ALL:
                    g, b, h, t, j = unit(n)
                    if n % UNITS == 0 and g >= 2:
                        dve.wait_ge(msp, g - 1)
                    dve.wait_ge(m_full, n + 1)
                    dve.tensor_reduce(mx[:, g % 2, t * GH + j:t * GH + j + 1], m_bank[n % M_BANKS][:, :], AX.X, ALU.max,
                                      negate=True).then_inc(m_done, 1)
                g, step = divmod(n - UNITS, UNITS)
                if 0 <= g < GROUPS and step < 4:
                    split_maxima(g, step)
                for st in STAGES_AT.get(s - 1, ()):
                    stage(*st)
                    if st[0] in ("K", "Q") and st[1] == 0:
                        split_projection(dve, link, 0, st[0], st[2])
                for (which, b), slot in NORM_SLOTS.items():
                    for t in range(QT):
                        if s == slot + t * norm_gap(which, b):
                            norm_statistics(which, b, t)
                for b, slot in ROUTE_SLOT.items():
                    if s == slot + 1:
                        route_sub(b)
                    for step in range(8):
                        if s == slot + 4 + step:
                            route(b, step)

            dve.wait_ge(ranks, 1)
            link(dve.tensor_scalar(cnt_i[:, :], s_bank[2][0:E, 0:1], float(P - 1), None, ALU.add))
            link(dve.tensor_scalar(cnt_i[:, :], cnt_i[:, :], P.bit_length() - 1, None, ALU.logical_shift_right))
            dve.tensor_copy(tiles_b[:, :], cnt_i[:, 0:1].to_broadcast([E, P])).then_inc(tiles_rdy, 1)
            dve.wait_ge(bases, 1)
            link(dve.tensor_scalar(tile_cmp[:, :], s_bank[2][:, 64 + E:64 + 2 * E], iota_p[:, 0:1], None, ALU.is_le))
            link(dve.tensor_reduce(tile_e[:, :], tile_cmp[:, :], AX.X, ALU.add))
            link(dve.tensor_scalar(base[:, :], s_bank[2][:, 64:64 + E], float(P), None, ALU.mult))
            dve.tensor_scalar(tile_eb[:, :], tile_e[:, :], float(E - 1), None, ALU.min).then_inc(tile_e_rdy, 1)
            link(dve.tensor_tensor(pos, misc[:, :].rearrange("p (t e) -> p t e", t=NT),
                                   base[:, :].unsqueeze(1).to_broadcast([P, NT, E]), ALU.add))
            p4 = prod.rearrange("p (t j e) -> p t j e", t=NT, j=TOPK)
            link(dve.tensor_tensor(p4, onehot[:, :, :, :], pos.unsqueeze(2).to_broadcast([P, NT, TOPK, E]), ALU.mult))
            link(dve.tensor_reduce(slot_f[:, :], prod.rearrange("p (n e) -> p n e", e=E), AX.X, ALU.add))
            link(dve.tensor_copy(slot_i[:, :], slot_f[:, :]))
            dve.tensor_scalar(xrow[:, :, M_SLOT:M_SLOT + TOPK], slot_f[:, :].rearrange("p (t j) -> p t j", j=TOPK),
                              1.0, None, ALU.add).then_inc(slots_rdy, 1)
            dve.wait_ge(tile_row, 1)
            dve.tensor_scalar(offs[:, :], s_bank[2][0:1, 256:256 + SLOT_TILES], float(WORDS), None, ALU.mult)\
                .then_inc(offs_rdy, 1)

            def shared_sum(b):
                dve.wait_ge(sd_full, SC * (b + 1))
                for i in range(2):
                    r = xres[:, b * QT + 2 * i:b * QT + 2 * i + 2, :]
                    dve.tensor_tensor(r, o_bank[i][:, :].rearrange("p (t n) -> p t n", t=2), r, ALU.add).then_inc(sd_out, 1)

            for k in range(B * SC):
                if k >= SC and k % SC == 1:
                    shared_sum(k // SC - 1)
                dve.wait_ge(sg_act, k + 1)
                if k >= SC:
                    dve.wait_ge(sd_full, k - SC + 1)
                dve.tensor_tensor(hid[:, k % SC, :], m_bank[k % 2][:, :], gated[k % 2], ALU.mult).then_inc(sg_hid, 1)
            shared_sum(B - 1)

            def destinations():
                dve.wait_ge(ld_meta, 16)
                shape = [P, SLOT_TILES, TOPK]
                link(dve.tensor_tensor(mine[:, :, :], meta[:, :, 0:TOPK], my_slot[:, :].unsqueeze(2).to_broadcast(shape),
                                       ALU.is_equal))
                dve.tensor_tensor(mtmp[:, :, :], mine[:, :, :], meta[:, :, TOPK:2 * TOPK], ALU.mult)
                link(dve.tensor_reduce(found[:, :], mine[:, :, :], AX.X, ALU.add))
                link(dve.tensor_reduce(wgt[:, :], mtmp[:, :, :], AX.X, ALU.add))
                link(dve.tensor_tensor(mtmp[:, :, :], mine[:, :, :], iota_j[:, :].unsqueeze(1).to_broadcast(shape), ALU.mult))
                link(dve.tensor_reduce(dest_f[:, :], mtmp[:, :, :], AX.X, ALU.add))
                link(dve.scalar_tensor_tensor(out=dest_f[:, :], in0=meta[:, :, 2 * TOPK], scalar=float(TOPK), in1=dest_f[:, :],
                                              op0=ALU.mult, op1=ALU.add))
                link(dve.tensor_tensor(dest_f[:, :], dest_f[:, :], dummy[:, :], ALU.subtract))
                link(dve.tensor_tensor(dest_f[:, :], dest_f[:, :], found[:, :], ALU.mult))
                dve.tensor_tensor(dest[:, :], dest_f[:, :], dummy[:, :], ALU.add).then_inc(dest_rdy, 1)

            def step(k, r):
                fixed = isinstance(k, int)
                if not fixed or k < SLOT_TILES:
                    dve.wait_ge(x_full, k + 1)
                    dve.tensor_copy(xT[r % 2], s_bank[r % 2][:, 0:D].rearrange("p (c t) -> p c t", c=C)).then_inc(x_rdy, 1)
                if not fixed or 1 <= k <= SLOT_TILES:
                    q = (r - 1) % 2
                    dve.wait_ge(g_act, k)
                    dve.tensor_tensor(hidden[q], m_bank[q][:, EH:2 * EH], gate[q], ALU.mult).then_inc(h_rdy, 1)

            for k in range(UNROLL):
                step(k, k)
                if k == 2:
                    destinations()
            with dve.Fori(1, SLOT_TILES // UNROLL) as i:
                for r in range(UNROLL):
                    step(i * UNROLL + r, r)
            step(SLOT_TILES, 0)

            for t in range(NT):
                z, a = zring[t % 4], zsum[t % 2]
                dve.wait_ge(ld_z[t % 4], 16 * (t // 4 + 1))
                link(dve.tensor_tensor(a, z[:, 0:2, :], z[:, 2:4, :], ALU.add))
                link(dve.tensor_tensor(a[:, 0, :], a[:, 0, :], a[:, 1, :], ALU.add))
                dve.tensor_tensor(xres[:, t, :], xres[:, t, :], a[:, 0, :], ALU.add).then_inc(z_sum, 1)


def kernel(x, ctx_1024, L0_xattn_Wk, L0_xattn_bk, L0_xattn_Wq, L0_xattn_bq, L0_xattn_Wc, L0_xattn_bc, L0_ffn_router_w,
           L0_ffn_router_bias, L0_ffn_gate_w, L0_ffn_up_w, L0_ffn_down_w, L0_ffn_sgate_w, L0_ffn_sup_w, L0_ffn_sdown_w):
    import numpy as np
    import concourse.bacc as bacc
    from concourse.bass_utils import run_bass_kernel_spmd

    def flat(a):
        return np.ascontiguousarray(np.asarray(a).reshape(N, D))

    def turned(a):
        return np.ascontiguousarray(np.asarray(a).T)

    def columns(a):
        return np.ascontiguousarray(np.asarray(a).reshape(C, P).T)

    def spread(a):
        return np.ascontiguousarray(np.broadcast_to(np.asarray(a), (P, a.shape[0])))

    gate, up, down = (np.asarray(a).transpose(2, 0, 1) for a in (L0_ffn_gate_w, L0_ffn_up_w, L0_ffn_down_w))
    wall = np.concatenate([m[c * P:(c + 1) * P] for c in range(C) for m in (gate, up)] + [down], axis=2)
    arrays = dict(
        x=flat(x), ctxn=flat(ctx_1024), ctxT=turned(flat(ctx_1024)),
        wkT=turned(L0_xattn_Wk), wqT=turned(L0_xattn_Wq), wcT=turned(L0_xattn_Wc),
        bk=columns(L0_xattn_bk), bq=columns(L0_xattn_bq), bc=spread(L0_xattn_bc),
        rwT=turned(L0_ffn_router_w), rb=spread(L0_ffn_router_bias),
        sgT=turned(L0_ffn_sgate_w), suT=turned(L0_ffn_sup_w), sdT=turned(L0_ffn_sdown_w),
        wall=np.ascontiguousarray(wall.reshape(P, E * WORDS)),
    )
    nc = bacc.Bacc("TRN2", target_bir_lowering=False, num_devices=1)
    aps = {n: nc.dram_tensor(f"in_{n}", a.shape, F32, kind="ExternalInput").ap() for n, a in arrays.items()}
    out = nc.dram_tensor("out_rows", (N, D), F32, kind="ExternalOutput").ap()
    build(nc, out=out, **aps)
    r = run_bass_kernel_spmd(nc, [{f"in_{n}": a for n, a in arrays.items()}], core_ids=[0])
    return r.results[0]["out_rows"].reshape(B, T, D)
```

```python
from contextlib import ExitStack

import concourse.bass as bass
from concourse import mybir

ALU = mybir.AluOpType
ACT = mybir.ActivationFunctionType
AX = mybir.AxisListType
F32 = mybir.dt.float32
BF16 = mybir.dt.bfloat16
I32 = mybir.dt.int32
U32 = mybir.dt.uint32

P = 128
B, T, D = 4, 512, 256
N = B * T
H, HD = 16, 16
C = D // P
QT = T // P
NT = N // P
E, EH, TOPK = 32, 128, 4
SH = 512
SC = SH // P
SCALE = HD ** -0.5
LN_EPS = 1e-5

Q_PART = (0, 0, 1, 0, 2, 1)
K_PART = (0, 1, 0, 2, 0, 1)
BLOCKS = len(Q_PART)
SHIFT_ROW = BLOCKS * HD
ROWS = SHIFT_ROW + 3

GH = 4
GROUPS = B * H // GH
BG = H // GH
UNITS = QT * GH
ALL = GROUPS * UNITS
AHEAD = 27
LAG = 4
S_BANKS, M_BANKS = 3, 3
P_RING = 8

UNROLL = 4
SLOT_TILES = -(-((N * TOPK + E * (P - 1)) // P) // UNROLL) * UNROLL
SLOTS = SLOT_TILES * P
FILL_LOADS = 8
WORDS = 3 * D
M_SLOT, M_WEIGHT, M_DEST, ROW = D, D + TOPK, D + 2 * TOPK, D + 3 * TOPK
REGION = N + P
NO_TOKENS = E * REGION
DEPTH = 2


def stage_plan():
    at = {}

    def put(slot, name, *arg):
        at.setdefault(slot, []).append((name, *arg))

    for u, stage in enumerate((("K", 0, 0), ("NT", 0, 0), ("NT", 0, 1), ("Q", 0, 0), ("K", 0, 1), ("Q", 0, 1))):
        put(-AHEAD - 6 + u, *stage)
    for u, stage in ((-27, ("NT", 1, 0)), (-25, ("NT", 1, 1)), (-22, ("K", 1, 0)), (-17, ("K", 1, 1)),
                     (-12, ("Q", 1, 0)), (-4, ("Q", 1, 1))):
        put(u, *stage)
    for b in range(2, B):
        s = UNITS * BG * (b - 1)
        for u, name, c in ((-32, "NT", 0), (-29, "NT", 1), (-16, "K", 0), (-5, "K", 1), (-2, "Q", 0), (3, "Q", 1)):
            put(s + u, name, b, c)
    for g in range(GROUPS):
        put(UNITS * g - 7, "MR", g)
        if g + 1 < GROUPS:
            put(UNITS * (g + 1) + 6, "YT", g)
    for b in range(B - 1):
        s = UNITS * BG * (b + 1)
        for u, name, c in ((11, "AT", 0), (14, "AT", 1), (19, "WC", 0), (27, "WC", 1),
                           (43, "XT", 0), (46, "XT", 1), (51, "LG", 0), (64, "RK", 0)):
            put(s + u, name, b, c)
    return at


SH_STEPS = B * SC
SH_BATCHES = 2
SH_UPS = (SH_BATCHES + 1) * SC
Z_RING = 12
POOL_TILES = (2, 5, 8, 11, 13)
VECTOR_TILES = [_t for _t in range(NT) if _t not in POOL_TILES]
SH_AT = {0: SH_UPS, 3: SH_UPS + 1, 6: SH_UPS + 2, 9: SH_UPS + 3}
SH_SUM_AT = {5: SH_BATCHES, 11: SH_BATCHES + 1}
GATES_AHEAD = 2
assert len(SH_AT) == SH_STEPS - SH_UPS and len(SH_SUM_AT) == B - SH_BATCHES

STAGES_AT = stage_plan()
FIRST_SLOT = min(STAGES_AT)
LAST_SLOT = ALL + LAG
ROUTE_SLOT = {b: UNITS * BG * (b + 1) + 51 for b in range(B - 1)}
ROUTE_STEPS = 8
PLACE_STEPS = 3
SCATTER_GAP = 3
LATE_STAGES = {0: ("YT", GROUPS - 1), 1: ("AT", B - 1, 0), 2: ("AT", B - 1, 1), 3: ("WC", B - 1, 0), 4: ("WC", B - 1, 1),
               6: ("XT", B - 1, 0), 7: ("XT", B - 1, 1), 8: ("LG", B - 1, 0), 10: ("RK", B - 1, 0)}
LATE_NORM, LATE_SCALING, LATE_ROUTE, LATE_COUNTS, LATE_BASES, LATE_TILES = 4, 5, 9, 10, 11, 13

OFFSETS_BOUNDED = "the tiles' experts were clamped to E - 1 before they were multiplied"

STAGE_NO = {}
for _s in range(FIRST_SLOT, LAST_SLOT + 1):
    for _st in STAGES_AT.get(_s, ()):
        STAGE_NO[_st] = len(STAGE_NO)
for _half in sorted(LATE_STAGES):
    STAGE_NO[LATE_STAGES[_half]] = len(STAGE_NO)


def through(*stage):
    return STAGE_NO[stage] + 1


SCATTER_SLOTS = [ROUTE_SLOT[_b] + 18 + SCATTER_GAP * _n for _b in range(B - 2) for _n in range(QT * TOPK)]
SCATTERED_EARLY = len(SCATTER_SLOTS)

NORM_SLOTS = {(1, 0): FIRST_SLOT, (1, 1): FIRST_SLOT + 3}
for _b in range(2, B):
    NORM_SLOTS[(1, _b)] = UNITS * BG * (_b - 1) - 45
for _b in range(B - 1):
    NORM_SLOTS[(2, _b)] = UNITS * BG * (_b + 1) + 29
NORM_NO = {k: n for n, k in enumerate(sorted(NORM_SLOTS, key=NORM_SLOTS.get))}
NORM_NO[(2, B - 1)] = len(NORM_NO)


def vector_scales(which, b):
    return (which, b) in ((1, 0), (2, B - 1))


def norm_gap(which, b):
    return int(which == 2 or b >= 2)


def unit(n):
    g, u = divmod(n, UNITS)
    t, j = divmod(u, GH)
    return g, g // BG, g % BG * GH + j, t, j


def build(nc, x, ctxn, ctxT, wkT, wqT, wcT, bk, bq, bc, rwT, rb, sgT, suT, sdT, wall, out):
    slot_rows = nc.dram_tensor("slot_rows", (NO_TOKENS + P, ROW), F32, kind="Internal").ap()
    choice_rows = nc.dram_tensor("choice_rows", (N * TOPK + SLOTS, D), F32, kind="Internal").ap()
    parts_d = nc.dram_tensor("parts", (B, 2, 3, D, T), BF16, kind="Internal").ap()
    with ExitStack() as ctx:
        def sb(name, shape, dt=F32):
            return ctx.enter_context(nc.sbuf_tensor(name, shape, dt))

        def ps(name, shape, dt=F32):
            return ctx.enter_context(nc.psum_tensor(name, shape, dt))

        def sem(name):
            return ctx.enter_context(nc.semaphore(name))

        weights = sb("weights", [P, E * WORDS])
        words = H * T // 2
        qs = [weights[:, i * words:(i + 1) * words].bitcast(BF16).rearrange("p (h t) -> p h t", h=H) for i in (0, 1)]
        ks = [weights[:, i * words:(i + 1) * words].bitcast(BF16).rearrange("p (h t) -> p h t", h=H) for i in (2, 3)]
        at = 4 * words
        vwords = QT * H * 32
        vaug = [weights[:, at + i * vwords:at + (i + 1) * vwords].rearrange("p (k h m) -> p k h m", k=QT, h=H)
                for i in (0, 1)]
        at += 2 * vwords
        expo = [weights[:, at + i * T:at + (i + 1) * T] for i in range(P_RING)]
        assert at + P_RING * T <= E * WORDS

        xres = sb("xres", [P, NT, D])
        xrow = sb("xrow", [P, NT, ROW])
        xn2T = sb("xn2T", [P, C, N])
        early = sb("early", [P, 6 * C * T])
        late = sb("late", [P, 4 * C * T])

        def cut(arena, sizes):
            at, got = 0, []
            for n in sizes:
                got.append(arena[:, at:at + n])
                at += n
            assert at <= arena.shape[1]
            return got

        def chunks(ap, n):
            return ap.rearrange("p (c n) -> p c n", c=n)

        cT, cn, xnT, full0, full1, rest, part0, part1 = cut(early, [C * T] * 3 + [T] * 3 + [3 * T // 2] * 2)
        cT, cn, xnT = chunks(cT, C), chunks(cn, QT), chunks(xnT, C)
        full = [full0, full1]
        part = [chunks(p.bitcast(BF16), 3) for p in (part0, part1)]
        o_sb, y, yT, wk, wq, wc = cut(late, [T, C * T, C * T, C * D, C * D, C * D])
        y, yT, wk, wq, wc = chunks(y, QT), chunks(yT, C), chunks(wk, C), chunks(wq, C), chunks(wc, C)

        sg, su, sd, gated0, gated1, hid = cut(early, [C * SH] * 2 + [SC * D] + [T] * 2 + [SC * T])
        sg, su, sd, hid = chunks(sg, C), chunks(su, C), chunks(sd, SC), chunks(hid, SC)
        gated = [gated0, gated1]
        xg, yo, xT0, xT1, *ring = cut(late, [UNROLL * ROW, UNROLL * D, C * P, C * P, P, P, P, P])
        xg, yo, xT = chunks(xg, UNROLL), chunks(yo, UNROLL), [chunks(xT0, C), chunks(xT1, C)]
        gate, hidden = ring[0:2], ring[2:4]
        gate_up = [chunks(g, 2 * C) for g in gated]
        zring = [chunks(z, TOPK) for z in cut(weights, [TOPK * D] * Z_RING)]
        zsum = [chunks(z, 2) for z in cut(weights, [TOPK * D] * Z_RING + [2 * D] * 4)[Z_RING:]]

        bk_s = sb("bk_s", [P, C])
        bq_s = sb("bq_s", [P, C])
        bc_s = sb("bc_s", [P, D])
        rw_s = sb("rw_s", [P, C, E])
        rb_s = sb("rb_s", [P, E])
        ident = sb("ident", [P, P])
        identb = sb("identb", [P, P], BF16)
        stats = sb("stats", [P, QT, 6])
        mv = sb("mv", [P, QT, 2])
        rstd = sb("rstd", [P, QT])
        minus_half = sb("minus_half", [P, QT])
        mx = sb("mx", [P, 2, UNITS])
        mres = sb("mres", [P, UNITS])
        msplit = sb("msplit", [P, QT, 3, GH], BF16)
        mrow = sb("mrow", [3 * GH, T], BF16)
        ones = sb("ones", [3, T], BF16)
        den = sb("den", [P, QT, GH])
        logits = sb("logits", [P, QT, E])
        top = sb("top", [P, QT, 8])
        top_i = sb("top_i", [P, QT, 8], U32)
        top_f = sb("top_f", [P, QT, TOPK])
        rstat = sb("rstat", [P, QT])
        onehot = sb("onehot", [P, QT, TOPK, E], BF16)
        mask = sb("mask", [P, B + 1, QT + 1, E], BF16)
        prod = sb("prod", [P, QT * TOPK, E])
        pos = sb("pos", [P, QT, E])
        zeros = sb("zeros", [P, ROW])
        iota_i = sb("iota_i", [P, SLOT_TILES], I32)
        iota_e = sb("iota_e", [P, E])
        iota_p = sb("iota_p", [P, 1])
        iota_j = sb("iota_j", [P, NT * TOPK], I32)
        region_e = sb("region_e", [P, E])
        region_p = sb("region_p", [E, 1])
        my_row = sb("my_row", [P, SLOT_TILES])
        dummy = sb("dummy_row", [P, SLOT_TILES])
        before = sb("before", [P, P], BF16)
        upto = sb("upto", [E, 2, E], BF16)
        onesb = sb("onesb", [P, P], BF16)
        cnt_i = sb("cnt_i", [E, 1], I32)
        tiles_b = sb("tiles_b", [E, P], BF16)
        fill_f = sb("fill_f", [E, 1])
        fill_i = sb("fill_i", [1, E], I32)
        tile_cmp = sb("tile_cmp", [P, E])
        tile_e = sb("tile_e", [P, 1])
        tile_0 = sb("tile_0", [P, 1])
        tile_r = sb("tile_r", [P, 1])
        tile_ok = sb("tile_ok", [P, 1])
        tile_rb = sb("tile_rb", [P, P])
        tile_row_i = sb("tile_row_i", [1, SLOT_TILES], I32)
        tile_eb = sb("tile_eb", [P, 1], BF16)
        offs = sb("offs", [1, SLOT_TILES], I32)
        slot_f = sb("slot_f", [P, NT * TOPK])
        slot_i = sb("slot_i", [P, NT * TOPK], I32)
        chosen = sb("chosen", [P, SLOT_TILES, 2])
        dest = sb("dest", [P, SLOT_TILES], I32)
        mine = sb("mine", [P, 2, TOPK])
        both = sb("both", [P, 2, 2, TOPK])
        dest_k = [sb(f"dest_k{i}", [P, 1], I32) for i in range(UNROLL)]

        s_bank = [ps(f"s_bank{i}", [P, T]) for i in range(S_BANKS)]
        m_bank = [ps(f"m_bank{i}", [P, T]) for i in range(M_BANKS)]
        o_bank = [ps("o_bank", [P, T]), m_bank[2]]
        misc = ps("misc", [P, T])
        miscb = misc[:, :].bitcast(BF16)

        ld_x = [sem(f"ld_x{b}") for b in range(B)]
        ld_cT = sem("ld_cT")
        ld_cn = sem("ld_cn")
        ld_wk = sem("ld_wk")
        ld_wq = sem("ld_wq")
        ld_b = sem("ld_b")
        ld_wc = sem("ld_wc")
        idents = sem("idents")
        ones_rdy = sem("ones_rdy")
        ones_in = sem("ones_in")
        norm1 = sem("norm1")
        misc_full = sem("misc_full")
        misc_free = sem("misc_free")
        full_rdy = sem("full_rdy")
        split = sem("split")
        parts_out = [sem(f"parts_out{i}") for i in range(2)]
        opnd = [sem(f"opnd{i}") for i in range(2)]
        opnd_first = [sem(f"opnd_first{c}") for c in range(C)]
        v_rdy = sem("v_rdy")
        m_full = sem("m_full")
        m_done = sem("m_done")
        msp = sem("msp")
        shift = [sem(f"shift{i}") for i in range(2)]
        s_full = sem("s_full")
        exp_done = sem("exp_done")
        pv_done = sem("pv_done")
        o_rdy = sem("o_rdy")
        norm2 = sem("norm2")
        rstd_rdy = sem("rstd_rdy")
        scaled = sem("scaled")
        resid = sem("resid")
        var1 = sem("var1")
        dchain = sem("dchain")
        pchain = sem("pchain")
        stored = sem("stored")
        filled = sem("filled")
        ld_sh = sem("ld_sh")
        ld_w = sem("ld_w")
        zero_rdy = sem("zero_rdy")
        consts = sem("consts")
        r_sub = sem("r_sub")
        r_exp = sem("r_exp")
        mask_rdy = sem("mask_rdy")
        counts = sem("counts")
        tiles_rdy = sem("tiles_rdy")
        fill_rdy = sem("fill_rdy")
        bases = sem("bases")
        tile_rdy = sem("tile_rdy")
        tile_rows = sem("tile_rows")
        offs_rdy = sem("offs_rdy")
        slots_rdy = sem("slots_rdy")
        scattered = sem("scattered")
        meta_1 = sem("meta_1")
        meta_2 = sem("meta_2")
        meta_3 = sem("meta_3")
        meta_4 = sem("meta_4")
        sg_full = sem("sg_full")
        sg_act = sem("sg_act")
        sg_hid = sem("sg_hid")
        sd_full = sem("sd_full")
        sd_out = sem("sd_out")
        ld_xg = [sem(f"ld_xg{i}") for i in range(UNROLL)]
        x_full = sem("x_full")
        x_rdy = sem("x_rdy")
        w_rdy = sem("w_rdy")
        g_full = sem("g_full")
        g_act = sem("g_act")
        h_rdy = sem("h_rdy")
        y_full = sem("y_full")
        yo_rdy = sem("yo_rdy")
        dest_cp = sem("dest_cp")
        z_out = [sem(f"z_out{i}") for i in range(UNROLL)]
        ld_z = [sem(f"ld_z{i}") for i in range(Z_RING)]
        z_sum = sem("z_sum")
        pool_sum = sem("pool_sum")

        block = ctx.enter_context(nc.Block())

        def slots():
            return range(FIRST_SLOT, LAST_SLOT + 1)

        def projection_no(b, name, c):
            return 4 * b + ((name == "Q") + 2 * c if b == 0 else 2 * (name == "Q") + c)

        def split_projection(eng, link, b, name, c):
            n = projection_no(b, name, c)
            eng.wait_ge(misc_free, through(name, b, c))
            eng.wait_ge(full_rdy, n + 1)
            if n:
                eng.wait_ge(split, n)
            f, p = full[n % 2], part[n % 2]
            link(eng.tensor_tensor(rest[:, :], f[:, :], p[:, 0, :], ALU.subtract))
            link(eng.tensor_copy(p[:, 1, :], rest[:, :]))
            eng.tensor_tensor(p[:, 2, :], rest[:, :], p[:, 1, :], ALU.subtract).then_inc(split, 1)

        def load_numbers(eng, ap, top, why):
            return nc.values_load_multi_w_load_instructions(ap, engines=(eng.engine,), min_val=0, max_val=top,
                                                            skip_runtime_bounds_check_because=why)[1]

        def fill_last_tiles(eng, experts):
            eng.wait_ge(fill_rdy, 1)
            for e in experts[::FILL_LOADS]:
                for first in load_numbers(eng, fill_i[0:1, e:e + FILL_LOADS], NO_TOKENS - P, "an expert has at most N tokens"):
                    eng.dma_start(slot_rows[bass.ds(first, P), :], zeros[:, :]).then_inc(filled, 16)

        def wait_summed(eng, t):
            if t in POOL_TILES:
                eng.wait_ge(pool_sum, POOL_TILES.index(t) + 1)
            else:
                eng.wait_ge(z_sum, VECTOR_TILES.index(t) + 1)

        def sum_tile(eng, link, t, n, sums, done):
            z, a = zring[t % Z_RING], sums[n % 2]
            eng.wait_ge(ld_z[t % Z_RING], 16 * (t // Z_RING + 1))
            link(eng.tensor_tensor(a, z[:, 0:2, :], z[:, 2:4, :], ALU.add))
            link(eng.tensor_tensor(a[:, 0, :], a[:, 0, :], a[:, 1, :], ALU.add))
            eng.tensor_tensor(xres[:, t, :], xres[:, t, :], a[:, 0, :], ALU.add).then_inc(done, 1)

        @block.sync
        def _(sp):
            def load_ctx(b):
                if b:
                    sp.wait_ge(misc_full, through("K", b - 1, 1))
                sp.dma_start(cT[:, :, :], ctxT[:, b * T:(b + 1) * T].rearrange("(c p) t -> p c t", p=P)).then_inc(ld_cT, 16)

            def load_values(b):
                if b:
                    sp.wait_ge(v_rdy, b)
                sp.dma_start(cn[:, :, :], ctxn[b * T:(b + 1) * T, :].rearrange("(k p) d -> p k d", p=P)).then_inc(ld_cn, 16)

            def load_x(b):
                sp.dma_start(xres[:, b * QT:(b + 1) * QT, :],
                             x[b * T:(b + 1) * T, :].rearrange("(k p) d -> p k d", p=P)).then_inc(ld_x[b], 16)

            sp.dma_start(wk[:, :, :], wkT.rearrange("(c p) n -> p c n", p=P)).then_inc(ld_wk, 16)
            load_ctx(0)
            load_values(0)
            load_x(0)
            sp.dma_start(bk_s[:, :], bk).then_inc(ld_b, 16)
            sp.dma_start(bq_s[:, :], bq).then_inc(ld_b, 16)
            sp.dma_start(wq[:, :, :], wqT.rearrange("(c p) n -> p c n", p=P)).then_inc(ld_wq, 16)
            sp.wait_ge(ones_rdy, 1)
            for i in range(2):
                sp.dma_start(ks[i][SHIFT_ROW:ROWS, :, :], ones[:, :].unsqueeze(1).to_broadcast([3, H, T])).then_inc(ones_in, 16)
            load_x(1)
            load_x(2)
            load_x(3)
            sp.dma_start(wc[:, :, :], wcT.rearrange("(c p) n -> p c n", p=P)).then_inc(ld_wc, 16)
            sp.dma_start(bc_s[:, :], bc).then_inc(ld_wc, 16)
            sp.dma_start(rw_s[:, :, :], rwT.rearrange("(c p) n -> p c n", p=P)).then_inc(ld_wc, 16)
            sp.dma_start(rb_s[:, :], rb).then_inc(ld_wc, 16)

            def store_parts(b, name, c):
                n = projection_no(b, name, c)
                sp.wait_ge(split, n + 1)
                sp.dma_start(parts_d[b, int(name == "Q"), :, c * P:(c + 1) * P, :].rearrange("s p t -> p s t"),
                             part[n % 2][:, :, :]).then_inc(parts_out[n % 2], 16)

            def stack(b, name, c=None):
                n = projection_no(b, name, 1 if c is None else c)
                if c is None:
                    sp.wait_ge(parts_out[1 - n % 2], 8 * (n + 1))
                sp.wait_ge(parts_out[n % 2], 16 * (n // 2 + 1))
                if b >= 2:
                    sp.wait_ge(s_full, UNITS * BG * (b - 1))
                dst, which = (qs[b % 2], Q_PART) if name == "Q" else (ks[b % 2], K_PART)
                heads, cols = slice(0, H), slice(0, D)
                if c is not None:
                    heads, cols = slice(c * H // C, (c + 1) * H // C), slice(c * P, (c + 1) * P)
                for i, s in enumerate(which):
                    sp.dma_start(dst[i * HD:(i + 1) * HD, heads, :],
                                 parts_d[b, int(name == "Q"), s, cols].rearrange("(h d) t -> d h t", d=HD))\
                        .then_inc(opnd[b % 2] if c is None else opnd_first[c], 16)

            def shift_rows(g):
                b, gg = divmod(g, BG)
                sp.wait_ge(misc_free, through("MR", g))
                sp.dma_start(qs[b % 2][SHIFT_ROW:ROWS, gg * GH:(gg + 1) * GH, :], mrow[:, :]).then_inc(shift[g % 2], 16)

            for s in slots():
                for name, *arg in STAGES_AT.get(s, ()):
                    if name in ("K", "Q"):
                        b, c = arg
                        store_parts(b, name, c)
                        if (name, c) == ("K", 1) and b + 1 < B:
                            load_ctx(b + 1)
                        if b == 0:
                            stack(b, name, c)
                            if (name, c) == ("K", 1):
                                load_values(1)
                    if name == "MR":
                        shift_rows(*arg)
                if s == 8:
                    load_values(2)
                if s == UNITS * BG + 12:
                    load_values(3)
                if s == 12:
                    sp.wait_ge(zero_rdy, 1)
                    sp.dma_start(slot_rows[NO_TOKENS:NO_TOKENS + P, :], zeros[:, :]).then_inc(filled, 16)
                if s == UNITS * BG * (B - 2) + 20:
                    sp.wait_ge(misc_full, through("Q", B - 1, 1))
                    sp.wait_ge(v_rdy, B)
                    sp.wait_ge(split, 4 * B)
                    for i in range(2):
                        sp.wait_ge(parts_out[i], 16 * 2 * B)
                    sp.dma_start(sg, sgT.rearrange("(c p) n -> p c n", p=P)).then_inc(ld_sh, 16)
                    sp.dma_start(su, suT.rearrange("(c p) n -> p c n", p=P)).then_inc(ld_sh, 16)
                    sp.dma_start(sd, sdT.rearrange("(c p) n -> p c n", p=P)).then_inc(ld_sh, 16)
                if s == ALL:
                    sp.wait_ge(pv_done, ALL)
                    q = E * WORDS // 4
                    for i in range(4):
                        sp.dma_start(weights[:, i * q:(i + 1) * q], wall[:, i * q:(i + 1) * q]).then_inc(ld_w, 16)
                b, u = divmod(s, UNITS * BG)
                if 1 <= b + 1 < B and (b or u):
                    if u == 10:
                        stack(b + 1, "K")
                    if u == 15:
                        stack(b + 1, "Q")

            fill_last_tiles(sp, range(E))

            sp.wait_ge(offs_rdy, 1)
            sp.wait_ge(filled, 16 * (E + 1))
            sp.wait_ge(scattered, 16 * NT * TOPK)

            def tile_rows_from(k):
                return load_numbers(sp, tile_row_i[0:1, bass.ds(k, UNROLL)], NO_TOKENS, "a tile starts within its expert's rows")

            def load_rows(k, r, first):
                if not isinstance(k, int):
                    sp.wait_ge(x_full, k - UNROLL + 1)
                    sp.wait_ge(meta_2, k - UNROLL + 1)
                sp.dma_start(xg[:, r, :], slot_rows[bass.ds(first, P), :]).then_inc(ld_xg[r], 16)

            for k, first in enumerate(tile_rows_from(0)):
                load_rows(k, k, first)
            with sp.Fori(1, SLOT_TILES // UNROLL) as i:
                for r, first in enumerate(tile_rows_from(i * UNROLL)):
                    load_rows(i * UNROLL + r, r, first)

            for i in range(UNROLL):
                sp.wait_ge(z_out[i], 16 * (SLOT_TILES // UNROLL))
            for t in range(NT):
                if t >= Z_RING:
                    wait_summed(sp, t - Z_RING)
                first = SLOTS + t * P * TOPK
                sp.dma_start(zring[t % Z_RING], choice_rows[first:first + P * TOPK, :].rearrange("(p j) d -> p j d", j=TOPK))\
                    .then_inc(ld_z[t % Z_RING], 16)

        @block.tensor
        def _(pe):
            def stage(name, *arg):
                no = STAGE_NO[(name, *arg)]
                if no:
                    pe.wait_ge(misc_free, no)
                if name in ("K", "Q"):
                    b, c = arg
                    if name == "K":
                        pe.wait_ge(ld_cT, 16 * (b + 1))
                        pe.wait_ge(ld_wk, 16)
                    else:
                        pe.wait_ge(misc_free, through("NT", b, 1))
                        pe.wait_ge(ld_wq, 16)
                    w, act = (wk, cT) if name == "K" else (wq, xnT)
                    for i in range(C):
                        mm = pe.matmul(misc[:, :], w[:, i, c * P:(c + 1) * P], act[:, i, :], start=i == 0, stop=i == C - 1)
                elif name == "NT":
                    b, c = arg
                    pe.wait_ge(norm1, b + 1)
                    pe.wait_ge(idents, 1)
                    for t in range(QT):
                        mm = pe.transpose(misc[:, t * P:(t + 1) * P], xrow[:, b * QT + t, c * P:(c + 1) * P], ident[:, :])
                elif name == "MR":
                    pe.wait_ge(msp, arg[0] + 1)
                    pe.wait_ge(idents, 2)
                    for t in range(QT):
                        mm = pe.transpose(miscb[0:3 * GH, t * P:(t + 1) * P],
                                          msplit[:, t, :, :].rearrange("p s j -> p (s j)"), identb[:, :])
                elif name == "YT":
                    pe.wait_ge(o_rdy, arg[0] + 1)
                    for t in range(QT):
                        mm = pe.transpose(misc[:, t * P:(t + 1) * P], o_sb[:, t * P:(t + 1) * P], ident[:, :])
                elif name == "AT":
                    b, c = arg
                    pe.wait_ge(misc_free, through("YT", BG * b + BG - 1))
                    for t in range(QT):
                        mm = pe.transpose(misc[:, t * P:(t + 1) * P], y[:, t, c * P:(c + 1) * P], ident[:, :])
                elif name == "WC":
                    b, half = arg
                    pe.wait_ge(misc_free, through("AT", b, 1))
                    pe.wait_ge(ld_wc, 64)
                    for t in range(2):
                        for i in range(C):
                            k = (2 * half + t) * P
                            mm = pe.matmul(misc[:, t * D:(t + 1) * D], yT[:, i, k:k + P], wc[:, i, :],
                                           start=i == 0, stop=i == C - 1)
                elif name == "XT":
                    b, c = arg
                    pe.wait_ge(norm2, b + 1)
                    for t in range(QT):
                        mm = pe.transpose(misc[:, t * P:(t + 1) * P], xrow[:, b * QT + t, c * P:(c + 1) * P], ident[:, :])
                elif name == "LG":
                    b = arg[0]
                    pe.wait_ge(misc_free, through("XT", b, 1))
                    for t in range(QT):
                        for i in range(C):
                            k = (b * QT + t) * P
                            mm = pe.matmul(misc[:, t * E:(t + 1) * E], xn2T[:, i, k:k + P], rw_s[:, i, :],
                                           start=i == 0, stop=i == C - 1)
                elif name == "RK":
                    b = arg[0]
                    pe.wait_ge(mask_rdy, b + 1)
                    pe.wait_ge(consts, 1)
                    m = mask[:, b, :, :].rearrange("p t e -> p (t e)")
                    pe.matmul(misc[:, 0:QT * E], before[:, :], m[:, E:], start=True, stop=False)
                    for t in range(QT):
                        mm = pe.matmul(misc[:, t * E:QT * E], onesb[:, :], m[:, 0:(QT - t) * E], start=False, stop=t == QT - 1)
                mm.then_inc(misc_full, 1)

            for s in slots():
                if 0 <= s < ALL:
                    g, b, h, t, j = unit(s)
                    if s == 0:
                        pe.wait_ge(ones_in, 32)
                    if s % UNITS == 0:
                        pe.wait_ge(shift[g % 2], 16 * (g // 2 + 1))
                    if s >= S_BANKS:
                        pe.wait_ge(exp_done, s - S_BANKS + 1)
                    pe.matmul(s_bank[s % S_BANKS][:, :], ks[b % 2][0:ROWS, h, t * P:(t + 1) * P], qs[b % 2][0:ROWS, h, :],
                              start=True, stop=True).then_inc(s_full, 1)
                n = s + AHEAD
                if 0 <= n < ALL:
                    g, b, h, t, j = unit(n)
                    if b == 0 and g % (BG // C) == 0 and n % UNITS == 0:
                        pe.wait_ge(opnd_first[g // (BG // C)], 16 * 2 * BLOCKS)
                    if b and n % (UNITS * BG) == 0:
                        pe.wait_ge(opnd[b % 2], 16 * 2 * BLOCKS * ((b + 1) // 2))
                    if n >= M_BANKS:
                        pe.wait_ge(m_done, n - M_BANKS + 1)
                    pe.matmul(m_bank[n % M_BANKS][:, :], qs[b % 2][0:SHIFT_ROW, h, t * P:(t + 1) * P],
                              ks[b % 2][0:SHIFT_ROW, h, :], start=True, stop=True).then_inc(m_full, 1)
                late = (s - LAG) % UNITS if s >= LAG + UNITS else None
                for n in {0: (), 1: (s - LAG - 1, s - LAG)}.get(late, (s - LAG,)):
                    if 0 <= n < ALL:
                        g, b, h, t, j = unit(n)
                        if n % (UNITS * BG) == 0:
                            pe.wait_ge(v_rdy, b + 1)
                        if n % UNITS == 0 and g:
                            pe.wait_ge(o_rdy, g)
                        pe.wait_ge(exp_done, n + 1)
                        pe.matmul(o_bank[0][32 * j:32 * (j + 1), :], vaug[b % 2][:, t, h, :], expo[n % P_RING],
                                  start=t == 0, stop=t == QT - 1).then_inc(pv_done, 1)
                for st in STAGES_AT.get(s, ()):
                    stage(*st)

            small = s_bank[2]
            def beside(half):
                if half == LATE_COUNTS:
                    pe.wait_ge(mask_rdy, B)
                    pe.matmul(small[0:E, 0:1], mask[:, B, 0, :], onesb[:, 0:1], start=True, stop=True).then_inc(counts, 1)
                if half in LATE_STAGES:
                    stage(*LATE_STAGES[half])
                if half == LATE_BASES:
                    pe.wait_ge(tiles_rdy, 1)
                    pe.matmul(small[:, 64:64 + 2 * E], tiles_b[:, :], upto[:, :, :].rearrange("p a b -> p (a b)"),
                              start=True, stop=True)
                    pe.matmul(small[0:1, 128:128 + E], fill_f[:, :], ident[0:E, 0:E], start=True, stop=True).then_inc(bases, 1)
                if half == LATE_TILES:
                    pe.wait_ge(tile_rdy, 1)
                    n = slice(0, SLOT_TILES)
                    pe.matmul(small[0:1, 256:256 + SLOT_TILES], tile_eb[n, 0:1], identb[n, n], start=True, stop=True)
                    pe.matmul(small[:, 384:384 + SLOT_TILES], tile_rb[n, :], ident[n, n], start=True, stop=True)\
                        .then_inc(tile_rows, 1)

            def shared_up(k):
                b, c = divmod(k, SC)
                if k >= 2:
                    pe.wait_ge(sg_hid, k - 1)
                for w, bank in ((sg, s_bank[k % 2]), (su, m_bank[k % 2])):
                    for i in range(C):
                        mm = pe.matmul(bank[:, :], w[:, i, c * P:(c + 1) * P], xn2T[:, i, b * T:(b + 1) * T],
                                       start=i == 0, stop=i == C - 1)
                mm.then_inc(sg_full, 1)

            def shared_down(k):
                b, c = divmod(k, SC)
                pe.wait_ge(sg_hid, k + 1)
                if c == 0 and b:
                    pe.wait_ge(sd_out, 2 * b)
                for t in range(QT):
                    mm = pe.matmul(o_bank[t // 2][:, t % 2 * D:(t % 2 + 1) * D], hid[:, c, t * P:(t + 1) * P], sd[:, c, :],
                                   start=c == 0 and t % 2 == 0, stop=c == SC - 1, skip_group_check=True)
                mm.then_inc(sd_full, 1)

            pe.wait_ge(ld_sh, 48)
            pe.wait_ge(exp_done, ALL)
            pe.wait_ge(m_done, ALL)
            for k in range(SH_BATCHES * SC):
                shared_up(k)
                if k == 0:
                    pe.wait_ge(o_rdy, GROUPS)
                beside(2 * k)
                if k:
                    shared_down(k - 1)
                beside(2 * k + 1)
            shared_up(SH_BATCHES * SC)
            shared_down(SH_BATCHES * SC - 1)
            for k in range(SH_BATCHES * SC + 1, SH_UPS):
                shared_up(k)

            pe.wait_ge(sg_hid, SH_UPS)
            pe.wait_ge(offs_rdy, 1)
            pe.wait_ge(ld_w, 64)
            y_bank = [s_bank[2], misc]

            def load_offsets(k, n):
                return load_numbers(pe, offs[0:1, bass.ds(k, n)], (E - 1) * WORDS, OFFSETS_BOUNDED)

            def step(k, r, w):
                fixed = isinstance(k, int)
                if not fixed or k < SLOT_TILES:
                    pe.wait_ge(ld_xg[r], 16 * (k // UNROLL + 1) if fixed else (k - r) * (16 // UNROLL) + 16)
                    for i in range(C):
                        mm = pe.transpose(s_bank[r % 2][:, i * P:(i + 1) * P], xg[:, r, i * P:(i + 1) * P], ident[:, :])
                    mm.then_inc(x_full, 1)
                if not fixed or 1 <= k <= SLOT_TILES:
                    q = (r - 1) % 2
                    pe.wait_ge(w_rdy, k)
                    pe.wait_ge(x_rdy, k)
                    for a in range(2):
                        for i in range(C):
                            mm = pe.matmul(m_bank[q][:, a * P:(a + 1) * P], gate_up[q][:, 2 * i + a, :], xT[q][:, i, :],
                                           start=i == 0, stop=i == C - 1)
                    mm.then_inc(g_full, 1)
                if not fixed or k >= DEPTH:
                    q = r % 2
                    pe.wait_ge(h_rdy, k - 1)
                    if not fixed or k >= 4:
                        pe.wait_ge(yo_rdy, k - 3)
                    pe.matmul(y_bank[q][:, 0:D], hidden[q], weights[:, bass.ds(w + C * D, D)],
                              start=True, stop=True).then_inc(y_full, 1)

            w = load_offsets(0, UNROLL - DEPTH)
            for k in range(UNROLL):
                step(k, k, w[k - DEPTH] if k >= DEPTH else None)
            with pe.Fori(1, SLOT_TILES // UNROLL) as i:
                w = load_offsets(i * UNROLL - DEPTH, UNROLL)
                for r in range(UNROLL):
                    step(i * UNROLL + r, r, w[r])
            w = load_offsets(SLOT_TILES - DEPTH, DEPTH)
            for k in range(DEPTH):
                step(SLOT_TILES + k, k, w[k])

            pe.wait_ge(x_rdy, SLOT_TILES)
            down = SH_BATCHES * SC
            for k in range(SH_UPS, SH_STEPS):
                shared_up(k)
                for _ in range(2):
                    if down < k:
                        shared_down(down)
                        down += 1
            for k in range(down, SH_STEPS):
                shared_down(k)

        @block.scalar
        def _(act):
            def stage(name, *arg):
                if name in ("K", "Q"):
                    b, c = arg
                    n = projection_no(b, name, c)
                    act.wait_ge(misc_full, through(name, *arg))
                    if n == 0:
                        act.wait_ge(ld_b, 32)
                    if n >= 2:
                        act.wait_ge(split, n - 1)
                        act.wait_ge(parts_out[n % 2], 16 * (n // 2))
                    bias = (bk_s if name == "K" else bq_s)[:, c:c + 1]
                    act.activation(full[n % 2][:, :], misc[:, :], ACT.Identity, bias=bias).then_inc(full_rdy, 1)
                    act.activation(part[n % 2][:, 0, :], misc[:, :], ACT.Identity, bias=bias).then_inc(misc_free, 1)
                elif name == "NT":
                    b, c = arg
                    act.wait_ge(misc_full, through(name, *arg))
                    act.copy(xnT[:, c, :], misc[:, :]).then_inc(misc_free, 1)
                elif name == "AT":
                    b, c = arg
                    act.wait_ge(misc_full, through(name, *arg))
                    act.copy(yT[:, c, :], misc[:, :]).then_inc(misc_free, 1)
                elif name == "XT":
                    b, c = arg
                    act.wait_ge(misc_full, through(name, *arg))
                    act.copy(xn2T[:, c, b * T:(b + 1) * T], misc[:, :]).then_inc(misc_free, 1)

            def router_exp(b):
                act.wait_ge(r_sub, b + 1)
                act.activation(logits[:, :, :], logits[:, :, :], ACT.Exp).then_inc(r_exp, 1)

            for s in slots():
                g, u = divmod(s - LAG, UNITS)
                g -= 1
                if u == 0 and 0 <= g < GROUPS:
                    act.wait_ge(pv_done, UNITS * (g + 1))
                    if g:
                        act.wait_ge(misc_full, through("YT", g - 1))
                    act.copy(o_sb[:, :], o_bank[0][:, :]).then_inc(o_rdy, 1)
                if 0 <= s < ALL:
                    act.wait_ge(s_full, s + 1)
                    if s >= P_RING:
                        act.wait_ge(pv_done, s - P_RING + 1)
                    act.activation(expo[s % P_RING], s_bank[s % S_BANKS][:, :], ACT.Exp, scale=SCALE).then_inc(exp_done, 1)
                for st in STAGES_AT.get(s - 1, ()):
                    stage(*st)
                for b, slot in ROUTE_SLOT.items():
                    if s == slot + 2:
                        router_exp(b)

            def beside(half):
                if half in LATE_STAGES:
                    stage(*LATE_STAGES[half])
                if half == LATE_ROUTE:
                    router_exp(B - 1)

            def shared_gate(k):
                act.wait_ge(sg_full, k + 1)
                if k >= 2:
                    act.wait_ge(sg_hid, k - 1)
                act.activation(gated[k % 2], s_bank[k % 2][:, :], ACT.Silu).then_inc(sg_act, 1)

            for k in range(SH_UPS):
                shared_gate(k)
                beside(2 * k)
                beside(2 * k + 1)

            def load_offsets(k, n):
                return load_numbers(act, offs[0:1, bass.ds(k, n)], (E - 1) * WORDS, OFFSETS_BOUNDED)

            def place_gate_up(r, w):
                act.copy(gate_up[r % 2], weights[:, bass.ds(w, 2 * C * EH)].rearrange("p (c n) -> p c n", c=2 * C))\
                    .then_inc(w_rdy, 1)

            def step(k, r, w=None):
                fixed = isinstance(k, int)
                if not fixed or 1 <= k <= SLOT_TILES:
                    q = (r - 1) % 2
                    act.wait_ge(g_full, k)
                    act.activation(gate[q], m_bank[q][:, 0:EH], ACT.Silu).then_inc(g_act, 1)
                if not fixed or k >= DEPTH:
                    o = (r - DEPTH) % UNROLL
                    act.wait_ge(meta_3, k - 1)
                    act.wait_ge(y_full, k - 1)
                    if not fixed:
                        act.wait_ge(z_out[o], (k - r) * (16 // UNROLL) - (16 if r < DEPTH else 0))
                    elif k - DEPTH >= UNROLL:
                        act.wait_ge(z_out[o], 16 * ((k - DEPTH) // UNROLL))
                    act.activation(yo[:, o, :], [s_bank[2], misc][r % 2][:, 0:D], ACT.Copy,
                                   scale=chosen[:, bass.ds(k - DEPTH, 1), 0]).then_inc(yo_rdy, 1)
                if w is not None:
                    place_gate_up(r + 1, w)

            act.wait_ge(sg_hid, SH_UPS)
            act.wait_ge(offs_rdy, 1)
            act.wait_ge(ld_w, 64)
            place_gate_up(0, load_offsets(0, 1)[0])
            for i in range(2):
                w = load_offsets(i * UNROLL + 1, UNROLL)
                for r in range(UNROLL):
                    step(i * UNROLL + r, r, w[r])
            with act.Fori(2, SLOT_TILES // UNROLL - 1) as i:
                w = load_offsets(i * UNROLL + 1, UNROLL)
                for r in range(UNROLL):
                    step(i * UNROLL + r, r, w[r])
            w = list(load_offsets(SLOT_TILES - UNROLL + 1, UNROLL - 1))
            for k in range(SLOT_TILES - UNROLL, SLOT_TILES + DEPTH):
                step(k, k % UNROLL, w.pop(0) if w else None)

            gates = sorted(SH_AT)
            for t in range(NT):
                while gates and gates[0] - GATES_AHEAD <= t:
                    shared_gate(SH_AT[gates.pop(0)])
                wait_summed(act, t)
                act.dma_start(out[t * P:(t + 1) * P, :], xres[:, t, :]).then_inc(stored, 16)
            act.wait_ge(stored, 16 * NT)

        @block.gpsimd
        def _(pool):
            chain = [0]
            small = s_bank[2]

            def link(ins):
                chain[0] += 1
                ins.then_inc(pchain, 1)
                pool.wait_ge(pchain, chain[0])

            link(pool.memset(ident[:, :], 0.0))
            link(pool.affine_select(out=ident[:, :], in_=ident[:, :], compare_op=ALU.not_equal, fill=1.0, base=0,
                                    pattern=[[-1, P]], channel_multiplier=1))
            pool.tensor_copy(identb[:, :], ident[:, :]).then_inc(idents, 2)
            link(pool.memset(minus_half[:, :], -0.5))
            link(pool.memset(zeros[:, :], 0.0))
            pool.nop().then_inc(zero_rdy, 1)
            for i in range(2):
                link(pool.memset(vaug[i], 0.0))
                link(pool.memset(vaug[i][:, :, :, HD:HD + 1], 1.0))

            def values(b):
                pool.wait_ge(ld_cn, 16 * (b + 1))
                if b >= 2:
                    pool.wait_ge(pv_done, UNITS * BG * (b - 1))
                pool.tensor_copy(vaug[b % 2].rearrange("p k h m -> p (k h) m")[:, :, 0:HD],
                                 cn[:, :, :].rearrange("p k (h d) -> p (k h) d", h=H)).then_inc(v_rdy, 1)

            def constants():
                def indices(out, pattern, base, step):
                    n = out.shape[1]
                    i = iota_i[0:out.shape[0], 0:n]
                    link(pool.iota(i, pattern, base=base, channel_multiplier=step))
                    link(pool.tensor_copy(out, i))

                indices(iota_e[:, :], [[1, E]], 0, 0)
                indices(iota_p[:, :], [[1, 1]], 0, 1)
                indices(region_e[:, :], [[REGION, E]], 0, 0)
                indices(region_p[:, :], [[1, 1]], 0, REGION)
                indices(dummy[:, :], [[P, SLOT_TILES]], 0, 1)
                link(pool.iota(iota_j[:, :], [[P * TOPK, NT], [1, TOPK]], base=SLOTS, channel_multiplier=TOPK))
                link(pool.tensor_copy(xrow[:, :, M_DEST:M_DEST + TOPK], iota_j[:, :].rearrange("p (t j) -> p t j", j=TOPK)))
                link(pool.memset(mask[:, 0, 0, :], 0.0))
                link(pool.memset(onesb[:, :], 1.0))
                link(pool.affine_select(out=before[:, :], in_=onesb[:, :], compare_op=ALU.is_gt, fill=0.0, base=0,
                                        pattern=[[1, P]], channel_multiplier=-1))
                link(pool.affine_select(out=upto[:, 0, :], in_=onesb[0:E, 0:E], compare_op=ALU.is_gt, fill=0.0, base=0,
                                        pattern=[[1, E]], channel_multiplier=-1))
                pool.affine_select(out=upto[:, 1, :], in_=onesb[0:E, 0:E], compare_op=ALU.is_ge, fill=0.0, base=0,
                                   pattern=[[1, E]], channel_multiplier=-1).then_inc(consts, 1)

            def add_bias(b):
                r = xres[:, b * QT:(b + 1) * QT, :]
                pool.tensor_tensor(r, r, bc_s[:, :].rearrange("p (o n) -> p o n", o=1).to_broadcast([P, QT, D]), ALU.add)\
                    .then_inc(resid, 1)

            def norm_scaling(which, b):
                no = NORM_NO[(which, b)]
                pool.wait_ge(var1, no + 1)
                link(pool.tensor_scalar(rstd[:, :], mv[:, :, 1], LN_EPS, None, ALU.add))
                power = pool.tensor_tensor(rstd[:, :], rstd[:, :], minus_half[:, :], ALU.pow)
                if vector_scales(which, b):
                    power.then_inc(rstd_rdy, 1)
                    if which == 1:
                        pool.wait_ge(norm1, 1)
                        pool.wait_ge(ld_wc, 64)
                        add_bias(0)
                    return
                link(power)
                if which == 2:
                    pool.wait_ge(misc_full, through("NT", b, 1))
                for t in range(QT):
                    last = pool.tensor_scalar(xrow[:, b * QT + t, 0:D], xres[:, b * QT + t, :], mv[:, t, 0:1],
                                              rstd[:, t:t + 1], ALU.subtract, ALU.mult)
                last.then_inc(norm1 if which == 1 else norm2, 1)
                pool.wait_ge(norm1 if which == 1 else norm2, b + 1)
                pool.nop().then_inc(scaled, 1)
                if which == 1:
                    add_bias(b)

            def scatter_tokens(n):
                t, j = divmod(n, TOPK)
                pool.wait_ge(slots_rdy, t // QT + 1)
                pool.indirect_dma_start(slot_rows, bass.IndirectOffsetOnAxis(ap=slot_i[:, n:n + 1], axis=0),
                                        xrow[:, t, :], None).then_inc(scattered, 16)

            for s in slots():
                if s == 2:
                    constants()
                if s in SCATTER_SLOTS:
                    scatter_tokens(SCATTER_SLOTS.index(s))
                for (which, b), slot in NORM_SLOTS.items():
                    if s == slot + (QT // 2 + 1) * norm_gap(which, b):
                        norm_scaling(which, b)
                for name, *arg in STAGES_AT.get(s, ()):
                    if name in ("K", "Q") and arg[0]:
                        split_projection(pool, link, arg[0], name, arg[1])
                    if (name, *arg) == ("K", 0, 1):
                        values(0)
                    if (name, *arg) == ("K", 1, 1):
                        values(1)
                b, u = divmod(s, UNITS * BG)
                if u == LAG + 4 and b >= 1 and b + 1 < B:
                    values(b + 1)

            norm_scaling(2, B - 1)
            for n in range(SCATTERED_EARLY, NT * TOPK):
                scatter_tokens(n)

            def fetch_destinations(k, r):
                if not isinstance(k, int) or k >= UNROLL:
                    pool.wait_ge(z_out[r], k // UNROLL * 16 if isinstance(k, int) else (k - r) * (16 // UNROLL))
                pool.wait_ge(meta_4, k + 1)
                pool.tensor_copy(dest_k[r][:, :], dest[:, bass.ds(k, 1)]).then_inc(dest_cp, 1)

            def scatter(k, r):
                pool.wait_ge(yo_rdy, k + 1)
                pool.wait_ge(dest_cp, k + 1)
                if not isinstance(k, int) or k + 1 < SLOT_TILES:
                    fetch_destinations(k + 1, (r + 1) % UNROLL)
                pool.indirect_dma_start(choice_rows, bass.IndirectOffsetOnAxis(ap=dest_k[r][:, 0:1], axis=0),
                                        yo[:, r, :], None).then_inc(z_out[r], 16)

            fetch_destinations(0, 0)
            for k in range(UNROLL):
                scatter(k, k)
            with pool.Fori(1, SLOT_TILES // UNROLL - 1) as i:
                for r in range(UNROLL):
                    scatter(i * UNROLL + r, r)
            for k in range(SLOT_TILES - UNROLL, SLOT_TILES):
                scatter(k, k % UNROLL)

            for n, t in enumerate(POOL_TILES):
                pool.wait_ge(sd_out, 2 * (t // QT + 1))
                sum_tile(pool, link, t, n, zsum[2:4], pool_sum)

        @block.vector
        def _(dve):
            chain = [0]
            small = s_bank[2]

            def link(ins):
                chain[0] += 1
                ins.then_inc(dchain, 1)
                dve.wait_ge(dchain, chain[0])

            dve.memset(ones[:, :], 1.0).then_inc(ones_rdy, 1)

            def split_maxima(g, step):
                m = mx[:, g % 2, :].rearrange("p (t j) -> p t j", t=QT)
                r = mres[:, :].rearrange("p (t j) -> p t j", t=QT)
                if step == 0:
                    dve.wait_ge(m_done, UNITS * (g + 1))
                    if g:
                        dve.wait_ge(misc_full, through("MR", g - 1))
                        dve.wait_ge(msp, g)
                    link(dve.tensor_copy(msplit[:, :, 0, :], m))
                elif step == 1:
                    link(dve.tensor_tensor(r, m, msplit[:, :, 0, :], ALU.subtract))
                elif step == 2:
                    link(dve.tensor_copy(msplit[:, :, 1, :], r))
                else:
                    dve.tensor_tensor(msplit[:, :, 2, :], r, msplit[:, :, 1, :], ALU.subtract).then_inc(msp, 1)

            def norm_scaling(which, b):
                done = norm1 if which == 1 else norm2
                dve.wait_ge(rstd_rdy, which)
                for t in range(QT):
                    last = dve.tensor_scalar(xrow[:, b * QT + t, 0:D], xres[:, b * QT + t, :], mv[:, t, 0:1],
                                             rstd[:, t:t + 1], ALU.subtract, ALU.mult)
                last.then_inc(done, 1)
                dve.wait_ge(done, b + 1)

            def norm_statistics(which, b, t):
                no = NORM_NO[(which, b)]
                if t == 0:
                    if which == 1:
                        dve.wait_ge(ld_x[b], 16)
                    else:
                        dve.wait_ge(misc_free, through("WC", b, 1))
                last = dve.bn_stats(stats[:, t, :], xres[:, b * QT + t, :])
                if t == QT - 1:
                    link(last)
                    if no >= 2:
                        dve.wait_ge(scaled, no - 1)
                    for i in range(QT):
                        last = dve.bn_aggr(mv[:, i, :], stats[:, i, :])
                    last.then_inc(var1, 1)
                    if which == 1 and b == 0:
                        norm_scaling(which, b)

            def stage(name, *arg):
                if name == "MR":
                    g, = arg
                    dve.wait_ge(misc_full, through(name, *arg))
                    if g:
                        dve.wait_ge(shift[(g - 1) % 2], 16 * ((g - 1) // 2 + 1))
                    dve.tensor_copy(mrow[:, :], miscb[0:3 * GH, 0:T]).then_inc(misc_free, 1)
                elif name == "YT":
                    g, = arg
                    dve.wait_ge(misc_full, through(name, *arg))
                    o = misc[:, :].rearrange("p (t j m) -> p t j m", t=QT, j=GH)
                    link(dve.reciprocal(den[:, :, :], o[:, :, :, HD]))
                    gg = g % BG
                    dve.tensor_tensor(y[:, :, gg * GH * HD:(gg + 1) * GH * HD].rearrange("p t (j d) -> p t j d", j=GH),
                                      o[:, :, :, 0:HD], den[:, :, :].unsqueeze(3).to_broadcast([P, QT, GH, HD]), ALU.mult)\
                        .then_inc(misc_free, 1)
                elif name == "WC":
                    b, half = arg
                    dve.wait_ge(misc_full, through(name, *arg))
                    dve.wait_ge(resid, b + 1)
                    r = xres[:, b * QT + 2 * half:b * QT + 2 * half + 2, :]
                    dve.tensor_tensor(r, misc[:, :].rearrange("p (t n) -> p t n", t=2), r, ALU.add).then_inc(misc_free, 1)
                elif name == "LG":
                    b = arg[0]
                    dve.wait_ge(misc_full, through(name, *arg))
                    dve.tensor_tensor(logits[:, :, :], misc[:, 0:QT * E].rearrange("p (t e) -> p t e", t=QT),
                                      rb_s[:, :].unsqueeze(1).to_broadcast([P, QT, E]), ALU.add).then_inc(misc_free, 1)
                elif name == "RK":
                    b = arg[0]
                    dve.wait_ge(misc_full, through(name, *arg))
                    dve.tensor_tensor(pos[:, :, :], misc[:, 0:QT * E].rearrange("p (t e) -> p t e", t=QT),
                                      region_e[:, :].unsqueeze(1).to_broadcast([P, QT, E]), ALU.add).then_inc(misc_free, 1)

            def route_sub(b):
                dve.wait_ge(misc_free, through("LG", b, 0))
                lg, st = logits[:, :, :], rstat[:, :]
                link(dve.tensor_reduce(st, lg, AX.X, ALU.max))
                dve.tensor_tensor(lg, lg, st.unsqueeze(2).to_broadcast([P, QT, E]), ALU.subtract).then_inc(r_sub, 1)

            def route(b, step):
                tiles = slice(b * QT, (b + 1) * QT)
                lg, st = logits[:, :, :], rstat[:, :]
                oh = onehot[:, :, :, :].rearrange("p t j e -> p (t j) e")
                if step == 0:
                    dve.wait_ge(r_exp, b + 1)
                    if b == 0:
                        dve.wait_ge(consts, 1)
                    link(dve.tensor_reduce(st, lg, AX.X, ALU.add))
                    link(dve.reciprocal(st, st))
                elif step == 1:
                    link(dve.tensor_tensor(lg, lg, st.unsqueeze(2).to_broadcast([P, QT, E]), ALU.mult))
                elif step == 2:
                    for t in range(QT):
                        last = dve.max(top[:, t, :], logits[:, t, :])
                    link(last)
                elif step == 3:
                    for t in range(QT):
                        last = dve.max_index(top_i[:, t, :], top[:, t, :], logits[:, t, :])
                    link(last)
                elif step == 4:
                    dve.tensor_copy(top_f[:, :, :], top_i[:, :, 0:TOPK])
                    link(dve.tensor_reduce(st, top[:, :, 0:TOPK], AX.X, ALU.add))
                    link(dve.tensor_scalar(st, st, 1e-12, None, ALU.max))
                elif step == 5:
                    link(dve.reciprocal(st, st))
                    dve.tensor_tensor(xrow[:, tiles, M_WEIGHT:M_WEIGHT + TOPK], top[:, :, 0:TOPK],
                                      st.unsqueeze(2).to_broadcast([P, QT, TOPK]), ALU.mult)
                elif step == 6:
                    link(dve.tensor_tensor(oh, iota_e[:, :].unsqueeze(1).to_broadcast([P, QT * TOPK, E]),
                                           top_f[:, :, :].rearrange("p t j -> p (t j)").unsqueeze(2)
                                           .to_broadcast([P, QT * TOPK, E]), ALU.is_equal))
                elif step == 7:
                    with nc.allow_low_precision(reason="zeros and ones are exact"):
                        link(dve.tensor_reduce(mask[:, b, 1:, :], onehot[:, :, :, :].rearrange("p t j e -> p t e j"),
                                               AX.X, ALU.add))
                        dve.tensor_reduce(mask[:, b + 1, 0, :], mask[:, b, :, :].rearrange("p t e -> p e t"), AX.X, ALU.add)\
                            .then_inc(mask_rdy, 1)

            def place(b, step):
                n = slice(b * QT * TOPK, (b + 1) * QT * TOPK)
                if step == 0:
                    dve.wait_ge(misc_free, through("RK", b, 0))
                    link(dve.tensor_tensor(prod[:, :, :].rearrange("p (t j) e -> p t j e", j=TOPK), onehot[:, :, :, :],
                                           pos[:, :, :].unsqueeze(2).to_broadcast([P, QT, TOPK, E]), ALU.mult))
                elif step == 1:
                    link(dve.tensor_reduce(slot_f[:, n], prod[:, :, :], AX.X, ALU.add))
                elif step == 2:
                    dve.tensor_scalar(xrow[:, b * QT:(b + 1) * QT, M_SLOT:M_SLOT + TOPK],
                                      slot_f[:, n].rearrange("p (t j) -> p t j", j=TOPK), 1.0, None, ALU.add)
                    link(dve.tensor_copy(slot_i[:, n], slot_f[:, n]))
                    dve.nop().then_inc(slots_rdy, 1)

            for s in slots():
                for st in STAGES_AT.get(s - 1, ()):
                    if st[0] == "MR":
                        stage(*st)
                n = s + AHEAD
                if 0 <= n < ALL:
                    g, b, h, t, j = unit(n)
                    if n % UNITS == 0 and g >= 2:
                        dve.wait_ge(msp, g - 1)
                    dve.wait_ge(m_full, n + 1)
                    dve.tensor_reduce(mx[:, g % 2, t * GH + j:t * GH + j + 1], m_bank[n % M_BANKS][:, :], AX.X, ALU.max,
                                      negate=True).then_inc(m_done, 1)
                g, u = divmod(n - UNITS, UNITS)
                if 0 <= g < GROUPS and u < 2:
                    split_maxima(g, 2 * u)
                    split_maxima(g, 2 * u + 1)
                for st in STAGES_AT.get(s - 1, ()):
                    if st[0] != "MR":
                        stage(*st)
                    if st[0] in ("K", "Q") and st[1] == 0:
                        split_projection(dve, link, 0, st[0], st[2])
                for (which, b), slot in NORM_SLOTS.items():
                    for t in range(QT):
                        if s == slot + t // 2 * norm_gap(which, b):
                            norm_statistics(which, b, t)
                for b, slot in ROUTE_SLOT.items():
                    if s == slot + 1:
                        route_sub(b)
                    for step in range(ROUTE_STEPS):
                        if s == slot + 4 + step:
                            route(b, step)
                    for step in range(PLACE_STEPS):
                        if s == slot + 15 + step:
                            place(b, step)

            def beside(half):
                if half == LATE_COUNTS:
                    dve.wait_ge(counts, 1)
                    link(dve.tensor_scalar(cnt_i[:, :], small[0:E, 0:1], float(P - 1), None, ALU.add))
                    link(dve.tensor_scalar(cnt_i[:, :], cnt_i[:, :], P.bit_length() - 1, None, ALU.logical_shift_right))
                    dve.tensor_tensor(fill_f[:, :], small[0:E, 0:1], region_p[:, :], ALU.add)
                    link(dve.tensor_copy(tiles_b[:, :], cnt_i[:, 0:1].to_broadcast([E, P])))
                    dve.nop().then_inc(tiles_rdy, 1)
                if half in LATE_STAGES:
                    stage(*LATE_STAGES[half])
                if half == LATE_NORM:
                    for t in range(QT):
                        norm_statistics(2, B - 1, t)
                if half == LATE_SCALING:
                    norm_scaling(2, B - 1)
                if LATE_STAGES.get(half) == ("LG", B - 1, 0):
                    route_sub(B - 1)
                if half == LATE_ROUTE:
                    for step in range(ROUTE_STEPS):
                        route(B - 1, step)
                if LATE_STAGES.get(half) == ("RK", B - 1, 0):
                    for step in range(PLACE_STEPS):
                        place(B - 1, step)
                if half == LATE_BASES:
                    dve.wait_ge(bases, 1)
                    dve.tensor_copy(fill_i[:, :], small[0:1, 128:128 + E]).then_inc(fill_rdy, 1)
                    ends = small[:, 64 + E:64 + 2 * E]
                    link(dve.tensor_scalar(tile_cmp[:, :], ends, iota_p[:, 0:1], None, ALU.is_le))
                    dve.tensor_reduce(tile_e[:, :], tile_cmp[:, :], AX.X, ALU.add)
                    link(dve.tensor_tensor(tile_cmp[:, :], ends, tile_cmp[:, :], ALU.mult))
                    link(dve.tensor_reduce(tile_0[:, :], tile_cmp[:, :], AX.X, ALU.max))
                    dve.tensor_scalar(tile_ok[:, :], tile_e[:, :], float(E), None, ALU.is_lt)
                    link(dve.tensor_scalar(tile_e[:, :], tile_e[:, :], float(E - 1), None, ALU.min))
                    link(dve.tensor_tensor(tile_0[:, :], iota_p[:, :], tile_0[:, :], ALU.subtract))
                    dve.tensor_scalar(tile_r[:, :], tile_e[:, :], float(REGION), float(-NO_TOKENS), ALU.mult, ALU.add)
                    dve.tensor_copy(tile_eb[:, :], tile_e[:, :])
                    link(dve.tensor_scalar(tile_0[:, :], tile_0[:, :], float(P), None, ALU.mult))
                    link(dve.tensor_tensor(tile_r[:, :], tile_r[:, :], tile_0[:, :], ALU.add))
                    link(dve.tensor_tensor(tile_r[:, :], tile_r[:, :], tile_ok[:, :], ALU.mult))
                    dve.tensor_scalar(tile_rb[:, :], tile_r[:, 0:1].to_broadcast([P, P]), float(NO_TOKENS), None, ALU.add)\
                        .then_inc(tile_rdy, 1)
                if half == LATE_TILES:
                    dve.wait_ge(tile_rows, 1)
                    rows = slice(384, 384 + SLOT_TILES)
                    dve.tensor_copy(tile_row_i[:, :], small[0:1, rows])
                    dve.tensor_scalar(my_row[:, :], small[:, rows], iota_p[:, 0:1], 1.0, ALU.add, ALU.add)
                    link(dve.tensor_scalar(offs[:, :], small[0:1, 256:256 + SLOT_TILES], float(WORDS), None, ALU.mult))
                    dve.nop().then_inc(offs_rdy, 1)

            def shared_sum(b):
                dve.wait_ge(sd_full, SC * (b + 1))
                for i in range(2):
                    r = xres[:, b * QT + 2 * i:b * QT + 2 * i + 2, :]
                    dve.tensor_tensor(r, o_bank[i][:, :].rearrange("p (t n) -> p t n", t=2), r, ALU.add).then_inc(sd_out, 1)

            def shared_hidden(k):
                dve.wait_ge(sg_act, k + 1)
                if k >= SC:
                    dve.wait_ge(sd_full, k - SC + 1)
                dve.tensor_tensor(hid[:, k % SC, :], m_bank[k % 2][:, :], gated[k % 2], ALU.mult).then_inc(sg_hid, 1)

            for k in range(SH_UPS):
                if k >= SC and k % SC == 1:
                    shared_sum(k // SC - 1)
                shared_hidden(k)
                beside(2 * k)
                beside(2 * k + 1)

            def step(k, r):
                fixed = isinstance(k, int)
                if not fixed or k < SLOT_TILES:
                    dve.wait_ge(ld_xg[r], 16 * (k // UNROLL + 1) if fixed else (k - r) * (16 // UNROLL) + 16)
                    dve.tensor_scalar(mine[:, r % 2, :], xg[:, r, M_SLOT:M_SLOT + TOPK], my_row[:, bass.ds(k, 1)], None,
                                      ALU.is_equal).then_inc(meta_1, 1)
                    dve.wait_ge(x_full, k + 1)
                    dve.tensor_copy(xT[r % 2], s_bank[r % 2][:, 0:D].rearrange("p (c t) -> p c t", c=C)).then_inc(x_rdy, 1)
                    dve.wait_ge(meta_1, k + 1)
                    dve.tensor_tensor(both[:, r % 2, :, :], xg[:, r, M_WEIGHT:ROW].rearrange("p (a j) -> p a j", a=2),
                                      mine[:, r % 2, :].unsqueeze(1).to_broadcast([P, 2, TOPK]), ALU.mult).then_inc(meta_2, 1)
                if not fixed or 1 <= k <= SLOT_TILES:
                    dve.wait_ge(meta_3, k)
                    dve.tensor_tensor(dest[:, bass.ds(k - 1, 1)], chosen[:, bass.ds(k - 1, 1), 1], dummy[:, bass.ds(k - 1, 1)],
                                      ALU.max).then_inc(meta_4, 1)
                    q = (r - 1) % 2
                    dve.wait_ge(g_act, k)
                    dve.tensor_tensor(hidden[q], m_bank[q][:, EH:2 * EH], gate[q], ALU.mult).then_inc(h_rdy, 1)
                if not fixed or k < SLOT_TILES:
                    dve.wait_ge(meta_2, k + 1)
                    dve.tensor_reduce(chosen[:, bass.ds(k, 1), :].rearrange("p o a -> p (o a)"), both[:, r % 2, :, :], AX.X,
                                      ALU.add).then_inc(meta_3, 1)

            for k in range(UNROLL):
                step(k, k)
            with dve.Fori(1, SLOT_TILES // UNROLL) as i:
                for r in range(UNROLL):
                    step(i * UNROLL + r, r)
            step(SLOT_TILES, 0)

            for t in range(NT):
                if t in SH_AT:
                    shared_hidden(SH_AT[t])
                if t in SH_SUM_AT:
                    shared_sum(SH_SUM_AT[t])
                if t in VECTOR_TILES:
                    sum_tile(dve, link, t, VECTOR_TILES.index(t), zsum[0:2], z_sum)


def kernel(x, ctx_1024, L0_xattn_Wk, L0_xattn_bk, L0_xattn_Wq, L0_xattn_bq, L0_xattn_Wc, L0_xattn_bc, L0_ffn_router_w,
           L0_ffn_router_bias, L0_ffn_gate_w, L0_ffn_up_w, L0_ffn_down_w, L0_ffn_sgate_w, L0_ffn_sup_w, L0_ffn_sdown_w):
    import numpy as np
    import concourse.bacc as bacc
    from concourse.bass_utils import run_bass_kernel_spmd

    def flat(a):
        return np.ascontiguousarray(np.asarray(a).reshape(N, D))

    def turned(a):
        return np.ascontiguousarray(np.asarray(a).T)

    def columns(a):
        return np.ascontiguousarray(np.asarray(a).reshape(C, P).T)

    def spread(a):
        return np.ascontiguousarray(np.broadcast_to(np.asarray(a), (P, a.shape[0])))

    gate, up, down = (np.asarray(a).transpose(2, 0, 1) for a in (L0_ffn_gate_w, L0_ffn_up_w, L0_ffn_down_w))
    wall = np.concatenate([m[c * P:(c + 1) * P] for c in range(C) for m in (gate, up)] + [down], axis=2)
    arrays = dict(
        x=flat(x), ctxn=flat(ctx_1024), ctxT=turned(flat(ctx_1024)),
        wkT=turned(L0_xattn_Wk), wqT=turned(L0_xattn_Wq), wcT=turned(L0_xattn_Wc),
        bk=columns(L0_xattn_bk), bq=columns(L0_xattn_bq), bc=spread(L0_xattn_bc),
        rwT=turned(L0_ffn_router_w), rb=spread(L0_ffn_router_bias),
        sgT=turned(L0_ffn_sgate_w), suT=turned(L0_ffn_sup_w), sdT=turned(L0_ffn_sdown_w),
        wall=np.ascontiguousarray(wall.reshape(P, E * WORDS)),
    )
    nc = bacc.Bacc("TRN2", target_bir_lowering=False, num_devices=1)
    aps = {n: nc.dram_tensor(f"in_{n}", a.shape, F32, kind="ExternalInput").ap() for n, a in arrays.items()}
    out = nc.dram_tensor("out_rows", (N, D), F32, kind="ExternalOutput").ap()
    build(nc, out=out, **aps)
    r = run_bass_kernel_spmd(nc, [{f"in_{n}": a for n, a in arrays.items()}], core_ids=[0])
    return r.results[0]["out_rows"].reshape(B, T, D)
```
